# Optimizing a Trainium2 kernel written in Bass

```python
import numpy as np
import jax
import jax.numpy as jnp

def _softmax(x, axis=-1):
    return jax.nn.softmax(x, axis=axis)

def _gelu(x):
    return jax.nn.gelu(x, approximate=True)

def _silu(x):
    return jax.nn.silu(x)

def _sigmoid(x):
    return jax.nn.sigmoid(x)

def _layernorm(x, axis=-1, eps=1e-05):
    m = jnp.mean(x, axis=axis, keepdims=True)
    v = jnp.var(x, axis=axis, keepdims=True)
    return (x - m) / jnp.sqrt(v + eps)

def _scatter_add(tgt, idx, src, axis=0):
    return tgt.at[idx].add(src)

def _segment_sum(src, seg, n):
    return jax.ops.segment_sum(src, seg, n)
kernel_name = 'mk_gnn_resnorm_d1_gnn_r8_7d9113'

def setup_inputs(seed: int=0):
    np.random.seed(seed)
    _w = jnp.asarray

    def _rec_inputs():
        import jax
        import jax.numpy as jnp
        _gk = jax.random.key(seed)
        x = -0.000202 + 1 * jax.random.normal(jax.random.fold_in(_gk, 1), (6250, 128), jnp.float32)
        src = jax.random.randint(jax.random.fold_in(_gk, 2), (100000,), 0, 6250, jnp.int32)
        dst = jax.random.randint(jax.random.fold_in(_gk, 3), (100000,), 0, 6250, jnp.int32)
        _o = jnp.argsort(dst, stable=True)
        src = src[_o]
        dst = dst[_o]
        edge_attr_10 = 0.000254407 + 0.99978 * jax.random.normal(jax.random.fold_in(_gk, 11), (100000, 10), jnp.float32)
        return (x, src, dst, edge_attr_10)
    x, src, dst, edge_attr_10 = _rec_inputs()

    def _L0_gnn_setup():
        import jax, jax.numpy as jnp
        import numpy as np
        N_NODES = 6250
        N_EDGES = 100000
        NODE_DIM = 128
        EDGE_DIM = 10
        IN_DIM = 2 * NODE_DIM + EDGE_DIM
        BN_EPS = 1e-05
        key = jax.random.key(seed)
        ks = jax.random.split(key, 8)
        h = jax.random.normal(ks[0], (N_NODES, NODE_DIM), dtype=jnp.float32)
        edge_index = jax.random.randint(ks[1], (2, N_EDGES), 0, N_NODES, dtype=jnp.int64)
        edge_feat = jax.random.normal(ks[2], (N_EDGES, EDGE_DIM), dtype=jnp.float32)
        scale = 1.0 / np.sqrt(IN_DIM)
        gate_w = jax.random.normal(ks[3], (IN_DIM, NODE_DIM), dtype=jnp.float32) * scale
        gate_b = jax.random.normal(ks[4], (NODE_DIM,), dtype=jnp.float32) * scale
        cand_w = jax.random.normal(ks[5], (IN_DIM, NODE_DIM), dtype=jnp.float32) * scale
        cand_b = jax.random.normal(ks[6], (NODE_DIM,), dtype=jnp.float32) * scale
        bn_gamma = jnp.ones((NODE_DIM,), dtype=jnp.float32)
        bn_beta = jnp.zeros((NODE_DIM,), dtype=jnp.float32)
        return {'h': h, 'edge_index': edge_index, 'edge_feat': edge_feat, 'gate_w': gate_w, 'gate_b': gate_b, 'cand_w': cand_w, 'cand_b': cand_b, 'bn_gamma': bn_gamma, 'bn_beta': bn_beta}
    _L0_gnn_all = _L0_gnn_setup()
    _L0_gnn_in = {k: v for k, v in _L0_gnn_all.items() if k in ('gate_w', 'gate_b', 'cand_w', 'cand_b', 'bn_gamma', 'bn_beta')}
    del _L0_gnn_all
    return {'x': x, 'src': src, 'dst': dst, 'edge_attr_10': edge_attr_10, 'L0_gnn_gate_w': _L0_gnn_in['gate_w'], 'L0_gnn_gate_b': _L0_gnn_in['gate_b'], 'L0_gnn_cand_w': _L0_gnn_in['cand_w'], 'L0_gnn_cand_b': _L0_gnn_in['cand_b'], 'L0_gnn_bn_gamma': _L0_gnn_in['bn_gamma'], 'L0_gnn_bn_beta': _L0_gnn_in['bn_beta']}

def reference(x, src, dst, edge_attr_10, L0_gnn_gate_w, L0_gnn_gate_b, L0_gnn_cand_w, L0_gnn_cand_b, L0_gnn_bn_gamma, L0_gnn_bn_beta):
    import jax
    import jax.numpy as jnp

    def _L0_gnn_ref(h, edge_index, edge_feat, gate_w, gate_b, cand_w, cand_b, bn_gamma, bn_beta):
        import jax, jax.numpy as jnp
        import numpy as np
        N_NODES = 6250
        N_EDGES = 100000
        NODE_DIM = 128
        EDGE_DIM = 10
        IN_DIM = 2 * NODE_DIM + EDGE_DIM
        BN_EPS = 1e-05
        src = edge_index[0]
        dst = edge_index[1]
        z = jnp.concatenate([h[src], h[dst], edge_feat], axis=1)
        g = jax.nn.sigmoid(z @ gate_w + gate_b)
        c = jax.nn.softplus(z @ cand_w + cand_b)
        m = g * c
        agg = jax.ops.segment_sum(m, src, num_segments=h.shape[0])
        mean = jnp.mean(agg, axis=0)
        var = jnp.var(agg, axis=0)
        agg_bn = (agg - mean) * jax.lax.rsqrt(var + BN_EPS) * bn_gamma + bn_beta
        return jax.nn.softplus(h + agg_bn)
    edge_index = jnp.stack([src, dst])
    x = _layernorm(x + _L0_gnn_ref(x, edge_index, edge_attr_10, L0_gnn_gate_w, L0_gnn_gate_b, L0_gnn_cand_w, L0_gnn_cand_b, L0_gnn_bn_gamma, L0_gnn_bn_beta), axis=-1)
    return x

_drawn_inputs = setup_inputs


def setup_inputs(seed=0):
    import zlib

    import numpy as np

    out = dict(_drawn_inputs(seed))
    spreads = {'L0_gnn_bn_gamma': (1.0, 0.2), 'L0_gnn_bn_beta': (0.0, 0.1)}
    factors = {'L0_gnn_gate_b': 8.0, 'L0_gnn_cand_b': 8.0}
    for name, (base, spread) in spreads.items():
        noise = np.random.default_rng([zlib.crc32(name.encode()), seed]).standard_normal(out[name].shape)
        drawn = base * np.exp(spread * noise) if base else spread * noise
        out[name] = jnp.asarray(drawn.astype(out[name].dtype))
    for name, factor in factors.items():
        out[name] = (out[name] * factor).astype(out[name].dtype)
    return out
```

```python
from contextlib import ExitStack

import concourse.bass as bass
from concourse import mybir

P = 128
ALU = mybir.AluOpType
ACT = mybir.ActivationFunctionType
F32 = mybir.dt.float32
BF16 = mybir.dt.bfloat16
I32 = mybir.dt.int32
U32 = mybir.dt.uint32
AX_X = mybir.AxisListType.X

BN_EPS = 1e-5
LN_EPS = 1e-5


def gnn_kernel(nc, x, src, dst, edge_attr, gate_w, gate_b, cand_w, cand_b, gamma, beta, out):
    N, D = x.shape
    E, A = edge_attr.shape
    D2 = 2 * D
    NB = -(-N // P)
    LAST = N - (NB - 1) * P
    assert D == P and NB % 2 == 1 and NB % 7 == 0

    CH = 17
    EP = -(-E // (P * 2 * CH)) * 2 * CH
    TAIL = E - (P - 1) * EP
    assert 0 < TAIL <= EP
    STAGES = EP // CH
    COLS = [(0, 6 * CH), (6 * CH, EP)]

    REC = A + 2
    LO, DST = A, A + 1
    G = 4
    RING = 4
    OHR = 8
    tiles = (E + NB * (P - 1)) // P
    GROUPS = -(-tiles // (G * OHR)) * OHR
    T = GROUPS * G
    ITERS = GROUPS // OHR
    GROWS = G * P
    SPARE = T * P
    assert EP - TAIL <= P
    GH = G.bit_length() - 1
    FILL = 8
    FROWS = T // FILL

    NCH = 7
    CB = NB // NCH
    CW = CB * D

    with ExitStack() as ctx:
        def sb(name, shape, dt=F32):
            return ctx.enter_context(nc.sbuf_tensor(name, shape, dt))

        def psum(name, shape, dt=F32):
            return ctx.enter_context(nc.psum_tensor(name, shape, dt))

        def sem(name):
            return ctx.enter_context(nc.semaphore(name))

        records = nc.dram_tensor("records", [SPARE + GROWS * P // G, REC], F32, kind="Internal").ap()
        dst_table = nc.dram_tensor("dst_table", [NB * P, D2], F32, kind="Internal").ap()

        ident = sb("ident", [P, P])
        below = sb("below", [P, P])
        upto = sb("upto", [P, P])
        ones = sb("ones", [P, P])
        node_iota = sb("node_iota", [P, P])
        tile_iota = sb("tile_iota", [NB, T])
        w_src = sb("w_src", [P, D2])
        w_dst = sb("w_dst", [P, D2])
        w_edge = sb("w_edge", [A + 1, D2])
        gamma_row = sb("gamma_row", [1, D2])
        gb = sb("gb", [P, D2])
        src_i = sb("src_i", [P, EP], I32)
        dst_i = sb("dst_i", [P, EP], I32)
        lo_i = sb("lo_i", [P, EP], I32)
        lo_f = sb("lo_f", [P, EP])
        hi_f = sb("hi_f", [P, EP], BF16)
        eq = sb("eq", [P, EP], mybir.dt.int16)
        eqb = sb("eqb", [P, EP], BF16)
        cum = sb("cum", [P, EP])
        pos = sb("pos", [P, EP])
        row_i = sb("row_i", [P, EP], I32)
        count = sb("count", [P, NB])
        first = sb("first", [P, NB])
        total_f = sb("total_f", [NB, 1])
        total_i = sb("total_i", [NB, 1], I32)
        block_tiles = sb("block_tiles", [NB, 1])
        block_end = sb("block_end", [NB, 1])
        tiles_below = sb("tiles_below", [NB, NB])
        begun = sb("begun", [NB, T])
        tile_block = sb("tile_block", [1, T], I32)
        stage = sb("stage", [P, 2, CH, REC])
        stage_row = sb("stage_row", [P, 2, CH], I32)
        fill = sb("fill", [P, FROWS, REC])
        x_in = sb("x_in", [P, 2, D])
        x_t = sb("x_t", [P, 2, D])
        src_table = sb("src_table", [P, NB * D2])
        dst_out = sb("dst_out", [P, 2, D2])
        shared = sb("shared", [P, EP * A])
        attr = shared[:, :].rearrange("p (t a) -> p t a", a=A)
        rec = sb("rec", [P, RING, G, REC])
        dst_rows = sb("dst_rows", [P, RING, G, D2])
        hot = sb("hot", [P, OHR, G * P])
        hot_t = sb("hot_t", [P, 2, G * P])
        attr_t = sb("attr_t", [A + 1, 2, G * P])
        GW = G * D2
        z = shared[:, 0:2 * GW].rearrange("p (s w) -> p s w", s=2)
        neg = shared[:, 2 * GW:4 * GW].rearrange("p (s w) -> p s w", s=2)
        parts = shared[:, 4 * GW:6 * GW].rearrange("p (s w) -> p s w", s=2)
        message = shared[:, 6 * GW:7 * GW].rearrange("p (s w) -> p s w", s=2)
        assert 7 * GW <= EP * A
        agg = sb("agg", [P, NB * D])
        xs = src_table[:, 0:NB * D]
        sq = src_table[:, NB * D:2 * NB * D]
        mean = sb("mean", [P, D])
        rstd = sb("rstd", [P, D])
        node_mean = sb("node_mean", [P, NB])
        node_rstd = sb("node_rstd", [P, NB])

        z_ps = psum("z_ps", [P, 2, GW])
        hot_ps = psum("hot_ps", [P, G * P])
        attr_ps = psum("attr_ps", [P, G * P])
        sum_ps = psum("sum_ps", [P, 2, G * D])

        S = {}

        def mk(*names):
            for n in names:
                S[n] = sem(n)
            return [S[n] for n in names]

        (src_loaded, dst_loaded, attr_loaded, weights_loaded, consts_ready, seq_done) = mk(
            "src_loaded", "dst_loaded", "attr_loaded", "weights_loaded", "consts_ready", "seq_done")
        (cleared, src_split, counted, ranked, rows_ready, base_ps, base_step) = mk(
            "cleared", "src_split", "counted", "ranked", "rows_ready", "base_ps", "base_step")
        (filled, staged, taken_up, tile_blocks_ready, gb_ps, gb_ready) = mk(
            "filled", "staged", "taken_up", "tile_blocks_ready", "gb_ps", "gb_ready")
        scattered = [sem(f"scattered{i}") for i in range(2)]
        x_loaded = [sem(f"x_loaded{i}") for i in range(2)]
        dst_stored = [sem(f"dst_stored{i}") for i in range(2)]
        (x_turned, x_t_ready, table_ps, table_out) = mk("x_turned", "x_t_ready", "table_ps", "table_out")
        rec_loaded = [sem(f"rec_loaded{i}") for i in range(RING)]
        gathered = [sem(f"gathered{i}") for i in range(RING)]
        (hot_ready, turned, hot_t_ready, z_done, z_added, logs_ready, parts_ready, gate_ready,
         message_ready, summed, agg_added) = mk(
            "hot_ready", "turned", "hot_t_ready", "z_done", "z_added", "logs_ready", "parts_ready",
            "gate_ready", "message_ready", "summed", "agg_added")
        (xs_loaded, col_sum, mean_ready, centered, squared, sq_sum, var_ready, std_ready, f_neg, f_log, f_y,
         f_sq, f_rstd, f_out, out_stored, nstep) = mk(
            "xs_loaded", "col_sum", "mean_ready", "centered", "squared", "sq_sum", "var_ready", "std_ready", "f_neg",
            "f_log", "f_y", "f_sq", "f_rstd", "f_out", "out_stored", "nstep")

        def after(eng, semaphore, value):
            if not isinstance(value, int) or value > 0:
                eng.wait_ge(semaphore, value)

        def steps(eng, lag, step):
            for u in range(OHR):
                step(0, u)
            with eng.Fori(1, ITERS) as it:
                for u in range(OHR):
                    step(it * OHR, u)
            for u in range(lag):
                step(GROUPS, u)

        def live(base, u, lag):
            return not isinstance(base, int) or 0 <= base + u - lag < GROUPS

        def fills(base, u, lag, inc):
            return base * (inc // RING) + ((u - lag) // RING + 1) * inc

        block = ctx.enter_context(nc.Block())

        @block.sync
        def _(sp):
            sp.wait_ge(cleared, 1)
            sp.dma_start(src_i[0:P - 1, :], src[0:(P - 1) * EP].rearrange("(p t) -> p t", t=EP)).then_inc(src_loaded, 16)
            sp.dma_start(src_i[P - 1:P, 0:TAIL], src[(P - 1) * EP:E].rearrange("(p t) -> p t", p=1)).then_inc(src_loaded, 16)

            def table_block(nb, b, rows=P):
                after(sp, x_turned, nb - 1)
                sp.dma_start(x_in[0:rows, b, :], x[bass.ds(nb * P, rows), :]).then_inc(x_loaded[b], 16)

            def table_store(nb, b):
                sp.wait_ge(table_out, nb * 2 + 2)
                sp.dma_start(dst_table[bass.ds(nb * P, P), :], dst_out[:, b, :]).then_inc(dst_stored[b], 16)

            table_block(0, 0)
            table_block(1, 1)
            sp.wait_ge(cleared, 4)
            sp.dma_start(dst_i[0:P - 1, :], dst[0:(P - 1) * EP].rearrange("(p t) -> p t", t=EP)).then_inc(dst_loaded, 16)
            sp.dma_start(dst_i[P - 1:P, 0:TAIL], dst[(P - 1) * EP:E].rearrange("(p t) -> p t", p=1)).then_inc(dst_loaded, 16)
            sp.dma_start(shared[0:P - 1, :], edge_attr[0:(P - 1) * EP, :].rearrange("(p t) a -> p (t a)", t=EP)).then_inc(attr_loaded, 16)
            sp.dma_start(shared[P - 1:P, 0:TAIL * A], edge_attr[(P - 1) * EP:E, :].rearrange("(p t) a -> p (t a)", p=1)).then_inc(attr_loaded, 16)

            with sp.Fori(0, (NB - 3) // 2) as i:
                table_block(i * 2 + 2, 0)
                table_store(i * 2, 0)
                table_block(i * 2 + 3, 1)
                table_store(i * 2 + 1, 1)
            table_block(NB - 1, 0, LAST)
            table_store(NB - 3, 0)
            table_store(NB - 2, 1)
            table_store(NB - 1, 0)

            for i in range(2):
                sp.wait_ge(scattered[i], 16 * EP // 2)
            rec_in = records[0:SPARE, :].rearrange("(g p j) c -> g p (j c)", p=P, j=G)

            def load_records(base, u):
                g, r = base + u, u % RING
                after(sp, z_added, g - RING + 1)
                sp.dma_start(rec[:, r, :, :].rearrange("p j c -> p (j c)"),
                             rec_in[bass.ds(g, 1)].rearrange("g p w -> (g p) w")).then_inc(rec_loaded[r], 16)

            steps(sp, 0, load_records)

            sp.wait_ge(z_done, GROUPS)
            sp.dma_start(xs[:, 0:(NB - 1) * D].rearrange("p (b d) -> p b d", d=D),
                         x[0:(NB - 1) * P, :].rearrange("(b p) d -> p b d", p=P)).then_inc(xs_loaded, 16)
            sp.dma_start(xs[0:LAST, (NB - 1) * D:NB * D], x[(NB - 1) * P:N, :]).then_inc(xs_loaded, 16)
            for c in range(NCH):
                sp.wait_ge(f_out, c + 1)
                b0, b1 = c * CB, min((c + 1) * CB, NB - 1)
                sp.dma_start(out[b0 * P:b1 * P, :].rearrange("(b p) d -> p b d", p=P),
                             agg[:, b0 * D:b1 * D].rearrange("p (b d) -> p b d", d=D)).then_inc(out_stored, 16)
            sp.dma_start(out[(NB - 1) * P:N, :], agg[0:LAST, (NB - 1) * D:NB * D]).then_inc(out_stored, 16)
            sp.wait_ge(out_stored, 16 * (NCH + 1))
            for b in range(2):
                sp.wait_ge(dst_stored[b], 16 * ((NB + 1 - b) // 2))

        @block.gpsimd
        def _(pool):
            pool.iota(node_iota[:, :], pattern=[[1, P]], base=0, channel_multiplier=0,
                      allow_small_or_imprecise_dtypes=True).then_inc(consts_ready, 1)
            pool.iota(tile_iota[:, :], pattern=[[1, T]], base=0, channel_multiplier=0,
                      allow_small_or_imprecise_dtypes=True).then_inc(consts_ready, 1)
            pool.iota(pos[:, :], pattern=[[1, EP]], base=SPARE - TAIL, channel_multiplier=0,
                      allow_small_or_imprecise_dtypes=True).then_inc(consts_ready, 1)
            pool.memset(ones[:, :], 1.0).then_inc(consts_ready, 1)
            pool.memset(attr_t[:, :, :], 1.0).then_inc(consts_ready, 1)
            pool.wait_ge(consts_ready, 5)
            pool.affine_select(out=ident[:, :], in_=ones[:, :], compare_op=ALU.is_equal, fill=0.0, base=0,
                               pattern=[[-1, P]], channel_multiplier=1).then_inc(consts_ready, 1)
            pool.affine_select(out=below[:, :], in_=ones[:, :], compare_op=ALU.is_gt, fill=0.0, base=0,
                               pattern=[[1, P]], channel_multiplier=-1).then_inc(consts_ready, 1)
            pool.affine_select(out=upto[:, :], in_=ones[:, :], compare_op=ALU.is_ge, fill=0.0, base=0,
                               pattern=[[1, P]], channel_multiplier=-1).then_inc(consts_ready, 1)

            pool.wait_ge(filled, 16 * FILL)

            with pool.Fori(0, STAGES // 2) as i:
                for h in range(2):
                    pool.wait_ge(staged, i * 8 + (h * 4 + 4))
                    pool.sem_inc(taken_up, 1)
                    for c in range(CH):
                        pool.indirect_dma_start(
                            out=records, out_offset=bass.IndirectOffsetOnAxis(ap=stage_row[:, h, c:c + 1], axis=0),
                            in_=stage[:, h, c, :], in_offset=None).then_inc(scattered[h], 16)

            def gather(g, r, it):
                pool.wait_ge(rec_loaded[r], it)
                pool.sem_inc(taken_up, 1)
                for j in range(G):
                    pool.indirect_dma_start(
                        out=dst_rows[:, r, j, :], out_offset=None, in_=dst_table,
                        in_offset=bass.IndirectOffsetOnAxis(ap=rec[:, r, j, DST:DST + 1].bitcast(I32), axis=0),
                    ).then_inc(gathered[r], 16)

            for b in range(2):
                pool.wait_ge(dst_stored[b], 16 * ((NB + 1 - b) // 2))

            with pool.Fori(0, GROUPS // RING) as it:
                for r in range(RING):
                    gather(it * RING + r, r, it * 16 + 16)

        @block.scalar
        def _(act):
            for k, (w, b) in enumerate(((gate_w, gate_b), (cand_w, cand_b))):
                cols = slice(k * D, (k + 1) * D)
                act.dma_start(w_src[:, cols], w[0:D, :]).then_inc(weights_loaded, 16)
                act.dma_start(w_dst[:, cols], w[D:2 * D, :]).then_inc(weights_loaded, 16)
                act.dma_start(w_edge[0:A, cols], w[2 * D:2 * D + A, :]).then_inc(weights_loaded, 16)
                act.dma_start(w_edge[A:A + 1, cols], b.rearrange("(a d) -> a d", a=1)).then_inc(weights_loaded, 16)
            act.dma_start(gamma_row[:, 0:D], gamma.rearrange("(a d) -> a d", a=1)).then_inc(weights_loaded, 16)
            act.dma_start(gamma_row[:, D:D2], beta.rearrange("(a d) -> a d", a=1)).then_inc(weights_loaded, 16)
            act.wait_ge(cleared, 2)
            rec_fill = records[0:SPARE, :].rearrange("(i p r) c -> i p (r c)", p=P, r=FROWS)
            for i in range(FILL):
                act.dma_start(rec_fill[i], fill[:, :, :].rearrange("p r c -> p (r c)")).then_inc(filled, 16)

            def evacuate(nb, b, stored, rows=P):
                act.wait_ge(x_turned, nb + 1)
                nc.scalar.copy(x_t[:, b, 0:rows], hot_ps[:, b * P:b * P + rows]).then_inc(x_t_ready, 1)
                act.wait_ge(table_ps, nb + 1)
                nc.scalar.copy(src_table[:, bass.ds(nb * D2, D2)], z_ps[:, b, 0:D2]).then_inc(table_out, 1)
                after(act, dst_stored[b], stored)
                nc.scalar.copy(dst_out[:, b, :], z_ps[:, b, 512:512 + D2]).then_inc(table_out, 1)

            evacuate(0, 0, 0)
            evacuate(1, 1, 0)
            with act.Fori(1, (NB - 1) // 2) as i:
                evacuate(i * 2, 0, i * 16)
                evacuate(i * 2 + 1, 1, i * 16)
            evacuate(NB - 1, 0, NB // 2 * 16, LAST)

            act.wait_ge(dst_loaded, 32)
            act.wait_ge(attr_loaded, 32)

            def stage_columns(t0, h, i):
                after(act, scattered[h], i * (16 * CH))
                cols = bass.ds(t0, CH)
                nc.scalar.copy(stage[:, h, :, 0:A], attr[:, cols, :]).then_inc(staged, 1)
                nc.scalar.copy(stage[:, h, :, LO:LO + 1].rearrange("p t c -> p (t c)"), lo_f[:, cols]).then_inc(staged, 1)
                nc.scalar.copy(stage[:, h, :, DST:DST + 1].bitcast(I32).rearrange("p t c -> p (t c)"),
                               dst_i[:, cols]).then_inc(staged, 1)
                nc.scalar.copy(stage_row[:, h, :], row_i[:, cols]).then_inc(staged, 1)

            act.wait_ge(rows_ready, 1)
            first_stages = COLS[0][1] // CH
            for k in range(first_stages):
                stage_columns(k * CH, k % 2, k // 2)
            act.wait_ge(rows_ready, 2)
            with act.Fori(first_stages // 2, STAGES // 2) as i:
                for h in range(2):
                    stage_columns(i * (2 * CH) + h * CH, h, i)

            nc.scalar.preload_act_table_set("natural_log_exp_and_others")

            def step(base, u):
                s = base + u
                if live(base, u, 1):
                    act.wait_ge(turned, s)
                    after(act, z_done, s - 2)
                    b = (u - 1) % 2
                    nc.scalar.copy(hot_t[:, b, :], hot_ps[:, :])
                    nc.scalar.copy(attr_t[0:A, b, :], attr_ps[0:A, :]).then_inc(hot_t_ready, 1)
                if live(base, u, 3):
                    b = (u - 3) % 2
                    act.wait_ge(z_added, s - 2)
                    after(act, parts_ready, s - 4)
                    nc.scalar.activation(neg[:, b, :], z[:, b, :], ACT.Abs).then_inc(logs_ready, 1)
                    act.wait_ge(logs_ready, s * 3 - 8)
                    nc.scalar.activation(neg[:, b, :], neg[:, b, :], ACT.Exp, scale=-1.0).then_inc(logs_ready, 1)
                    act.wait_ge(logs_ready, s * 3 - 7)
                    nc.scalar.activation(neg[:, b, :], neg[:, b, :], ACT.Ln, bias=1.0).then_inc(logs_ready, 1)
                if live(base, u, 4):
                    b = (u - 4) % 2
                    act.wait_ge(parts_ready, s - 3)
                    gate = parts[:, b, :].rearrange("p (j d) -> p j d", d=D2)[:, :, 0:D]
                    nc.scalar.activation(gate, gate, ACT.Exp).then_inc(gate_ready, 1)

            steps(act, 4, step)

            for c in range(NCH):
                act.wait_ge(centered, c + 1)
                if c == 0:
                    act.wait_ge(col_sum, 1)
                nc.scalar.activation(sq[:, c * CW:(c + 1) * CW], agg[:, c * CW:(c + 1) * CW], ACT.Square).then_inc(squared, 1)
            act.wait_ge(var_ready, 1)
            nc.scalar.activation(rstd[:, :], rstd[:, :], ACT.Sqrt).then_inc(std_ready, 1)
            nc.scalar.preload_act_table_set("natural_log_exp_and_others")
            for c in range(NCH):
                part = sq[:, c * CW:(c + 1) * CW]
                act.wait_ge(f_neg, c + 1)
                nc.scalar.activation(part, part, ACT.Exp).then_inc(f_log, 1)
                act.wait_ge(f_log, 2 * c + 1)
                nc.scalar.activation(part, part, ACT.Ln, bias=1.0).then_inc(f_log, 1)
            for c in range(NCH):
                part = sq[:, c * CW:(c + 1) * CW]
                act.wait_ge(f_y, c + 1)
                nc.scalar.activation(part, agg[:, c * CW:(c + 1) * CW], ACT.Square).then_inc(f_sq, 1)
            act.wait_ge(f_rstd, 1)
            nc.scalar.activation(node_rstd[:, :], node_rstd[:, :], ACT.Sqrt).then_inc(f_rstd, 1)

        @block.vector
        def _(dve):
            v = nc.vector
            v.memset(src_i[:, :], NB * P).then_inc(cleared, 1)
            v.memset(fill[:, :, :], 0.0).then_inc(nstep, 1)
            dve.wait_ge(nstep, 1)
            v.memset(fill[:, :, LO:LO + 1], -1.0).then_inc(cleared, 1)
            v.memset(dst_i[96:P, TAIL:EP], 0).then_inc(cleared, 1)
            v.memset(shared[96:P, TAIL * A:EP * A], 0.0).then_inc(cleared, 1)

            dve.wait_ge(src_loaded, 32)
            v.tensor_scalar(lo_i[:, :], src_i[:, :], P - 1, None, ALU.bitwise_and).then_inc(src_split, 1)
            v.tensor_scalar(row_i[:, :], src_i[:, :], 7, None, ALU.logical_shift_right).then_inc(src_split, 1)
            dve.wait_ge(src_split, 2)
            v.tensor_copy(lo_f[:, :], lo_i[:, :]).then_inc(src_split, 1)
            v.tensor_copy(hi_f[:, :], row_i[:, :]).then_inc(src_split, 1)
            dve.wait_ge(src_split, 4)
            dve.wait_ge(consts_ready, 8)
            with dve.Fori(0, NB) as b:
                v.tensor_scalar(eqb[:, :], hi_f[:, :], node_iota[:, bass.ds(b, 1)], 0.0, ALU.is_equal, ALU.add,
                                accum_out=count[:, bass.ds(b, 1)]).then_inc(counted, 1)
                dve.wait_ge(counted, b + 1)
            v.memset(agg[:, :], 0.0).then_inc(nstep, 1)
            dve.wait_ge(base_ps, 1)
            v.tensor_scalar(total_f[:, :], attr_ps[0:NB, NB:NB + 1], float(P - 1), None, ALU.add).then_inc(base_step, 1)
            dve.wait_ge(base_step, 1)
            v.tensor_copy(total_i[:, :], total_f[:, :]).then_inc(base_step, 1)
            dve.wait_ge(base_step, 2)
            v.tensor_scalar(total_i[:, :], total_i[:, :], 7, None, ALU.logical_shift_right).then_inc(base_step, 1)
            dve.wait_ge(base_step, 3)
            v.tensor_copy(block_tiles[:, :], total_i[:, :]).then_inc(base_step, 1)
            dve.wait_ge(base_step, 4)
            v.tensor_scalar(tiles_below[:, :], below[0:NB, 0:NB], block_tiles[:, 0:1], None, ALU.mult).then_inc(base_step, 1)
            dve.wait_ge(base_ps, 2)
            v.tensor_scalar(first[:, :], attr_ps[:, 256:256 + NB], float(P), -1.0, ALU.mult, ALU.add).then_inc(base_step, 1)
            v.tensor_copy(block_end[:, :], attr_ps[0:NB, 256 + NB:257 + NB]).then_inc(base_step, 1)
            dve.wait_ge(base_step, 7)
            v.tensor_tensor(first[:, :], first[:, :], attr_ps[:, 0:NB], ALU.add).then_inc(base_step, 1)
            v.tensor_scalar(begun[:, :], tile_iota[:, :], block_end[:, 0:1], None, ALU.is_ge).then_inc(base_step, 1)
            dve.wait_ge(base_step, 9)

            for n, (t0, t1) in enumerate(COLS):
                w = t1 - t0
                with dve.Fori(0, NB) as b:
                    v.tensor_scalar(eq[:, t0:t1], hi_f[:, t0:t1], node_iota[:, bass.ds(b, 1)], None,
                                    ALU.is_equal).then_inc(ranked, 1)
                    dve.wait_ge(ranked, b * 4 + (n * NB * 4 + 1))
                    v.tensor_tensor_scan(cum[:, t0:t1], eq[:, t0:t1], eq[:, t0:t1], first[:, bass.ds(b, 1)],
                                         ALU.add, ALU.bypass).then_inc(ranked, 1)
                    dve.wait_ge(ranked, b * 4 + (n * NB * 4 + 2))
                    v.tensor_scalar(first[:, bass.ds(b, 1)], cum[:, t1 - 1:t1], 0.0, None, ALU.add).then_inc(ranked, 1)
                    v.copy_predicated(pos[:, t0:t1], eq[:, t0:t1], cum[:, t0:t1]).then_inc(ranked, 1)
                    dve.wait_ge(ranked, b * 4 + (n * NB * 4 + 4))
                done = n * 6
                v.tensor_copy(row_i[:, t0:t1], pos[:, t0:t1]).then_inc(nstep, 1)
                dve.wait_ge(nstep, done + 3)
                v.tensor_scalar(src_i[:, t0:t1], row_i[:, t0:t1], P - 1, GH, ALU.bitwise_and, ALU.logical_shift_left).then_inc(nstep, 1)
                v.tensor_scalar(lo_i[:, t0:t1], row_i[:, t0:t1], 7, G - 1, ALU.logical_shift_right, ALU.bitwise_and).then_inc(nstep, 1)
                v.tensor_scalar(row_i[:, t0:t1], row_i[:, t0:t1], 7 + GH, 7 + GH, ALU.logical_shift_right, ALU.logical_shift_left).then_inc(nstep, 1)
                dve.wait_ge(nstep, done + 6)
                v.tensor_tensor(row_i[:, t0:t1], row_i[:, t0:t1], src_i[:, t0:t1], ALU.bitwise_or).then_inc(nstep, 1)
                dve.wait_ge(nstep, done + 7)
                v.tensor_tensor(row_i[:, t0:t1], row_i[:, t0:t1], lo_i[:, t0:t1], ALU.bitwise_or).then_inc(nstep, 1)
                dve.wait_ge(nstep, done + 8)
                dve.sem_inc(rows_ready, 1)
                if n == 0:
                    dve.wait_ge(base_ps, 3)
                    v.tensor_scalar(tile_block[:, :].rearrange("p (k t) -> p k t", k=2), sum_ps[0:1, :, 0:T // 2], float(NB - 1), None, ALU.min).then_inc(tile_blocks_ready, 1)
                    dve.wait_ge(gb_ps, 1)
                    v.tensor_copy(gb[:, :], sum_ps[:, 0, 0:D2]).then_inc(gb_ready, 1)

            def step(base, u):
                s = base + u
                if live(base, u, 3):
                    r, b = (u - 3) % RING, (u - 3) % 2
                    dve.wait_ge(gathered[r], fills(base, u, 3, 16 * G))
                    dve.wait_ge(z_done, s - 2)
                    after(dve, parts_ready, s - 4)
                    v.tensor_tensor(z[:, b, :], z_ps[:, b, :], dst_rows[:, r, :, :].rearrange("p j d -> p (j d)"),
                                    ALU.add).then_inc(z_added, 1)
                if live(base, u, 0):
                    r = u % RING
                    dve.wait_ge(rec_loaded[r], fills(base, u, 0, 16))
                    after(dve, summed, s - OHR + 1)
                    v.tensor_tensor(hot[:, u, :].rearrange("p (j n) -> p j n", n=P),
                                    node_iota[:, :].unsqueeze(1).to_broadcast([P, G, P]),
                                    rec[:, r, :, LO:LO + 1].to_broadcast([P, G, P]), ALU.is_equal).then_inc(hot_ready, 1)
                if live(base, u, 4):
                    b = (u - 4) % 2
                    dve.wait_ge(logs_ready, s * 3 - 9)
                    after(dve, message_ready, s - 5)
                    for k, op in enumerate((ALU.min, ALU.max)):
                        def half(a):
                            return a[:, b, :].rearrange("p (j d) -> p j d", d=D2)[:, :, k * D:(k + 1) * D]
                        last = v.scalar_tensor_tensor(out=half(parts), in0=half(z), scalar=0.0, in1=half(neg), op0=op,
                                                      op1=ALU.add if k else ALU.subtract)
                    last.then_inc(parts_ready, 1)
                if live(base, u, 5):
                    b = (u - 5) % 2
                    dve.wait_ge(gate_ready, s - 4)
                    after(dve, summed, s - 6)
                    halves = parts[:, b, :].rearrange("p (j d) -> p j d", d=D2)
                    v.tensor_tensor(message[:, b, :].rearrange("p (j d) -> p j d", d=D), halves[:, :, 0:D],
                                    halves[:, :, D:D2], ALU.mult).then_inc(message_ready, 1)
                if live(base, u, 7):
                    dve.wait_ge(summed, s - 6)
                    for j in range(G):
                        at = nc.vector.value_load(tile_block[0:1, bass.ds((s - 7) * G + j, 1)], min_val=0, max_val=NB - 1)
                        after(dve, agg_added, (s - 7) * G + j)
                        part = agg[:, bass.ds(at * D, D)]
                        v.tensor_tensor(part, part, sum_ps[:, (u - 7) % 2, j * D:(j + 1) * D], ALU.add).then_inc(agg_added, 1)

            steps(dve, 7, step)

            dve.wait_ge(agg_added, T)
            base = 14
            dve.wait_ge(col_sum, 1)
            v.tensor_reduce(mean[:, :], sum_ps[:, 0, :].rearrange("p (c f) -> p f c", f=D), AX_X, ALU.add).then_inc(nstep, 1)
            dve.wait_ge(nstep, base + 1)
            v.tensor_scalar(mean[:, :], mean[:, :], 1.0 / N, None, ALU.mult).then_inc(mean_ready, 1)
            dve.wait_ge(mean_ready, 1)

            def blocks(a, c, w=CB):
                return a[:, c * CW:(c + 1) * CW].rearrange("p (b d) -> p b d", d=D)

            def every_block(a):
                return a.unsqueeze(1).to_broadcast([P, CB, D])

            for c in range(NCH):
                v.tensor_tensor(blocks(agg, c), blocks(agg, c), every_block(mean[:, :]), ALU.subtract).then_inc(centered, 1)
            dve.wait_ge(sq_sum, 1)
            v.tensor_reduce(rstd[:, :], sum_ps[:, 1, :].rearrange("p (c f) -> p f c", f=D), AX_X, ALU.add).then_inc(nstep, 1)
            dve.wait_ge(nstep, base + 2)
            v.tensor_scalar(rstd[:, :], rstd[:, :], 1.0 / N, BN_EPS, ALU.mult, ALU.add).then_inc(var_ready, 1)
            dve.wait_ge(std_ready, 1)
            v.reciprocal(rstd[:, :], rstd[:, :]).then_inc(nstep, 1)
            dve.wait_ge(nstep, base + 3)
            dve.wait_ge(gb_ready, 1)
            v.tensor_tensor(rstd[:, :], rstd[:, :], gb[:, 0:D], ALU.mult).then_inc(nstep, 1)
            dve.wait_ge(nstep, base + 4)
            dve.wait_ge(xs_loaded, 32)
            dve.wait_ge(squared, NCH)
            n = base + 4
            for c in range(NCH):
                a, xb = blocks(agg, c), blocks(xs, c)
                v.tensor_tensor(a, a, every_block(rstd[:, :]), ALU.mult).then_inc(nstep, 1)
                n += 1
                dve.wait_ge(nstep, n)
                v.tensor_tensor(a, a, every_block(gb[:, D:D2]), ALU.add).then_inc(nstep, 1)
                n += 1
                dve.wait_ge(nstep, n)
                v.tensor_tensor(a, a, xb, ALU.add).then_inc(nstep, 1)
                n += 1
                dve.wait_ge(nstep, n)
                t = agg[:, c * CW:(c + 1) * CW]
                v.scalar_tensor_tensor(out=sq[:, c * CW:(c + 1) * CW], in0=t, scalar=-1.0, in1=t, op0=ALU.mult,
                                       op1=ALU.min).then_inc(f_neg, 1)
            for c in range(NCH):
                a, xb, l = blocks(agg, c), blocks(xs, c), blocks(sq, c)
                mb = node_mean[:, c * CB:(c + 1) * CB]
                dve.wait_ge(f_log, 2 * c + 2)
                v.scalar_tensor_tensor(out=a, in0=a, scalar=0.0, in1=l, op0=ALU.max, op1=ALU.add).then_inc(nstep, 1)
                n += 1
                dve.wait_ge(nstep, n)
                v.tensor_tensor(a, a, xb, ALU.add).then_inc(nstep, 1)
                n += 1
                dve.wait_ge(nstep, n)
                v.tensor_reduce(mb, a, AX_X, ALU.add).then_inc(nstep, 1)
                n += 1
                dve.wait_ge(nstep, n)
                v.tensor_scalar(mb, mb, 1.0 / D, None, ALU.mult).then_inc(nstep, 1)
                n += 1
                dve.wait_ge(nstep, n)
                v.tensor_tensor(a, a, mb.unsqueeze(2).to_broadcast([P, CB, D]), ALU.subtract).then_inc(f_y, 1)
            for c in range(NCH):
                dve.wait_ge(f_sq, c + 1)
                v.tensor_reduce(node_rstd[:, c * CB:(c + 1) * CB], blocks(sq, c), AX_X, ALU.add).then_inc(nstep, 1)
                n += 1
            dve.wait_ge(nstep, n)
            v.tensor_scalar(node_rstd[:, :], node_rstd[:, :], 1.0 / D, LN_EPS, ALU.mult, ALU.add).then_inc(f_rstd, 1)
            dve.wait_ge(f_rstd, 2)
            v.reciprocal(node_rstd[:, :], node_rstd[:, :]).then_inc(nstep, 1)
            n += 1
            dve.wait_ge(nstep, n)
            for c in range(NCH):
                rb = node_rstd[:, c * CB:(c + 1) * CB]
                v.tensor_tensor(blocks(agg, c), blocks(agg, c), rb.unsqueeze(2).to_broadcast([P, CB, D]),
                                ALU.mult).then_inc(f_out, 1)

        @block.tensor
        def _(pe):
            def tables(nb, b, loads, rows=P):
                pe.wait_ge(x_loaded[b], loads)
                after(pe, x_t_ready, nb - 1)
                pe.transpose(hot_ps[:, b * P:b * P + rows], x_in[0:rows, b, :], ident[0:rows, 0:rows]).then_inc(x_turned, 1)
                pe.wait_ge(x_t_ready, nb + 1)
                after(pe, table_out, nb * 2 - 2)
                pe.matmul(z_ps[:, b, 0:D2], x_t[:, b, :], w_src[:, :], start=True, stop=True)
                pe.matmul(z_ps[:, b, 512:512 + D2], x_t[:, b, :], w_dst[:, :], start=True, stop=True).then_inc(table_ps, 1)

            pe.wait_ge(consts_ready, 8)
            pe.wait_ge(weights_loaded, 160)
            tables(0, 0, 16)
            tables(1, 1, 16)
            with pe.Fori(1, NB // 4) as i:
                tables(i * 2, 0, i * 16 + 16)
                tables(i * 2 + 1, 1, i * 16 + 16)

            pe.wait_ge(counted, NB)
            pe.matmul(attr_ps[:, 0:NB], below[:, :], count[:, :], start=True, stop=True)
            pe.matmul(attr_ps[0:NB, NB:NB + 1], count[:, :], ones[:, 0:1], start=True, stop=True).then_inc(base_ps, 1)
            pe.wait_ge(base_step, 5)
            pe.matmul(attr_ps[:, 256:256 + NB], ones[0:NB, :], tiles_below[:, :], start=True, stop=True)
            pe.matmul(attr_ps[0:NB, 256 + NB:257 + NB], upto[0:NB, 0:NB], block_tiles[:, :], start=True, stop=True).then_inc(base_ps, 1)
            pe.wait_ge(base_step, 9)
            for k in range(2):
                mm = pe.matmul(sum_ps[0:1, k, 0:T // 2], ones[0:NB, 0:1], begun[:, k * (T // 2):(k + 1) * (T // 2)],
                               start=True, stop=True)
            mm.then_inc(base_ps, 1)

            with pe.Fori(NB // 4, (NB - 1) // 2) as i:
                tables(i * 2, 0, i * 16 + 16)
                tables(i * 2 + 1, 1, i * 16 + 16)
            tables(NB - 1, 0, 16 * (NB // 2 + 1), LAST)

            pe.wait_ge(tile_blocks_ready, 1)
            pe.matmul(sum_ps[:, 0, 0:D2], ones[0:1, :], gamma_row[:, :], start=True, stop=True).then_inc(gb_ps, 1)
            pe.wait_ge(gb_ready, 1)
            pe.wait_ge(table_out, 2 * NB)

            def step(base, u):
                s = base + u
                if live(base, u, 1):
                    pe.wait_ge(hot_ready, s)
                    after(pe, hot_t_ready, s - 1)
                    for j in range(G):
                        pe.transpose(hot_ps[:, j * P:(j + 1) * P], hot[:, (u - 1) % OHR, j * P:(j + 1) * P], ident[:, :])
                        mm = pe.transpose(attr_ps[0:A, j * P:(j + 1) * P], rec[:, (u - 1) % RING, j, 0:A], ident[:, :])
                    mm.then_inc(turned, 1)
                if live(base, u, 2):
                    b = (u - 2) % 2
                    pe.wait_ge(hot_t_ready, s - 1)
                    after(pe, z_added, s - 3)
                    for j in range(G):
                        at = nc.tensor.value_load(tile_block[0:1, bass.ds((s - 2) * G + j, 1)], min_val=0, max_val=NB - 1)
                        to = z_ps[:, b, j * D2:(j + 1) * D2]
                        pe.matmul(to, attr_t[:, b, j * P:(j + 1) * P], w_edge[:, :], start=True, stop=False)
                        mm = pe.matmul(to, hot_t[:, b, j * P:(j + 1) * P], src_table[:, bass.ds(at * D2, D2)],
                                       start=False, stop=True)
                    mm.then_inc(z_done, 1)
                if live(base, u, 6):
                    pe.wait_ge(message_ready, s - 5)
                    after(pe, agg_added, (s - 7) * G)
                    o, b = (u - 6) % OHR, (u - 6) % 2
                    for j in range(G):
                        mm = pe.matmul(sum_ps[:, b, j * D:(j + 1) * D], hot[:, o, j * P:(j + 1) * P],
                                       message[:, b, j * D:(j + 1) * D], start=True, stop=True)
                    mm.then_inc(summed, 1)

            steps(pe, 6, step)

            def node_sums(a, to):
                full = (NB - 1) // G
                for c in range(full):
                    pe.matmul(to, ones[:, :], a[:, c * G * D:(c + 1) * G * D], start=(c == 0), stop=False)
                assert NB - 1 == full * G
                return pe.matmul(to[:, 0:D], ones[0:LAST, :], a[0:LAST, (NB - 1) * D:NB * D], start=False, stop=True)

            pe.wait_ge(agg_added, T)
            node_sums(agg, sum_ps[:, 0, :]).then_inc(col_sum, 1)
            pe.wait_ge(squared, NCH)
            node_sums(sq, sum_ps[:, 1, :]).then_inc(sq_sum, 1)


_INS = ['x', 'src', 'dst', 'edge_attr_10', 'L0_gnn_gate_w', 'L0_gnn_gate_b', 'L0_gnn_cand_w', 'L0_gnn_cand_b',
        'L0_gnn_bn_gamma', 'L0_gnn_bn_beta']


def kernel(**inputs):
    import numpy as _np
    import concourse.bacc as _bacc
    from concourse import mybir as _mybir
    from concourse.bass_utils import run_bass_kernel_spmd as _run

    nc = _bacc.Bacc("TRN2", target_bir_lowering=False, num_devices=1)
    arrays, args = {}, []
    for name in _INS:
        a = _np.ascontiguousarray(inputs[name])
        arrays[f"in_{name}_dram"] = a
        args.append(nc.dram_tensor(f"in_{name}_dram", a.shape, _mybir.dt.from_np(a.dtype), kind="ExternalInput").ap())
    shape = tuple(inputs['x'].shape)
    args.append(nc.dram_tensor("out_0_dram", shape, _mybir.dt.float32, kind="ExternalOutput").ap())
    gnn_kernel(nc, *args)
    r = _run(nc, [arrays], core_ids=[0])
    return r.results[0]["out_0_dram"]
```

```python
from contextlib import ExitStack

import concourse.bass as bass
from concourse import mybir

P = 128
ALU = mybir.AluOpType
ACT = mybir.ActivationFunctionType
F32 = mybir.dt.float32
BF16 = mybir.dt.bfloat16
I32 = mybir.dt.int32
U32 = mybir.dt.uint32
AX_X = mybir.AxisListType.X

BN_EPS = 1e-5
LN_EPS = 1e-5


def gnn_kernel(nc, x, src, dst, edge_attr, gate_w, gate_b, cand_w, cand_b, gamma, beta, out):
    N, D = x.shape
    E, A = edge_attr.shape
    D2 = 2 * D
    NB = -(-N // P)
    LAST = N - (NB - 1) * P
    assert D == P and NB % 2 == 1 and NB % 7 == 0

    CH = 17
    EP = -(-E // (P * 2 * CH)) * 2 * CH
    TAIL = E - (P - 1) * EP
    assert 0 < TAIL <= EP
    STAGES = EP // CH
    COLS = [(0, 6 * CH), (6 * CH, EP)]

    K = 6 * A
    LO = K // 2
    DST = LO + 1
    REC = DST + 1
    KB = K + 3
    G = 4
    RING = 4
    OHR = 8
    tiles = (E + NB * (P - 1)) // P
    GROUPS = -(-tiles // (G * OHR)) * OHR
    T = GROUPS * G
    ITERS = GROUPS // OHR
    GROWS = G * P
    SPARE = T * P
    assert EP - TAIL <= P
    GH = G.bit_length() - 1
    FILL = 8
    FROWS = T // FILL

    NCH = 7
    CB = NB // NCH
    CW = CB * D

    with ExitStack() as ctx:
        def sb(name, shape, dt=F32):
            return ctx.enter_context(nc.sbuf_tensor(name, shape, dt))

        def psum(name, shape, dt=F32):
            return ctx.enter_context(nc.psum_tensor(name, shape, dt))

        def sem(name):
            return ctx.enter_context(nc.semaphore(name))

        records = nc.dram_tensor("records", [SPARE + GROWS * P // G, REC], F32, kind="Internal").ap()
        dst_table = nc.dram_tensor("dst_table", [NB * P, D2], F32, kind="Internal").ap()

        ident = sb("ident", [P, P])
        below = sb("below", [P, P])
        upto = sb("upto", [P, P])
        ones = sb("ones", [P, P])
        node_iota = sb("node_iota", [P, P])
        tile_iota = sb("tile_iota", [NB, T])
        w_src = sb("w_src", [P, D2])
        w_dst = sb("w_dst", [P, D2])
        w_edge = sb("w_edge", [A + 1, D2])
        w_parts = sb("w_parts", [A + 1, 3, D2], BF16)
        w_stack = sb("w_stack", [KB, D2], BF16)
        ident_bf = sb("ident_bf", [P, P], BF16)
        minus_ident = sb("minus_ident", [P, P], BF16)
        gamma_row = sb("gamma_row", [1, D2])
        gb = sb("gb", [P, D2])
        ranking = sb("ranking", [P, 7 * EP])
        def rank_buf(k, dt=F32):
            return ranking[:, k * EP:(k + 1) * EP] if dt is F32 else ranking[:, k * EP:(k + 1) * EP].bitcast(dt)

        src_i, dst_i, lo_i, row_i = (rank_buf(k, I32) for k in range(4))
        lo_f, pos, spare = (rank_buf(k) for k in (4, 5, 6))
        hi_f = sb("hi_f", [P, EP], BF16)
        count = sb("count", [P, NB])
        first = sb("first", [P, NB])
        total_f = sb("total_f", [NB, 1])
        total_i = sb("total_i", [NB, 1], I32)
        block_tiles = sb("block_tiles", [NB, 1])
        block_end = sb("block_end", [NB, 1])
        tiles_below = sb("tiles_below", [NB, NB])
        begun = sb("begun", [NB, T])
        tile_block = sb("tile_block", [1, GROUPS, G])
        BITS = (NB - 1).bit_length()
        assert BITS * G <= 24
        packed = sb("packed", [1, GROUPS])
        group_blocks = sb("group_blocks", [1, GROUPS], I32)
        stage = sb("stage", [P, 2, CH, REC])
        stage_row = sb("stage_row", [P, 2, CH], I32)
        x_in = sb("x_in", [P, RING, D])
        x_t = sb("x_t", [P, 2, D])
        src_parts = sb("src_parts", [P, NB * 3 * D2], BF16)
        dst_out = sb("dst_out", [P, RING, D2])
        shared = sb("shared", [P, EP * A])
        attr = shared[:, :].rearrange("p (t a) -> p t a", a=A)
        rec = sb("rec", [P, RING, G, REC])
        assert RING * G * D2 + G * P <= 7 * EP
        hot_t = ranking[:, 7 * EP - G * P:].bitcast(BF16).rearrange("p (b n) -> p b n", b=2)
        dst_rows = ranking[:, 0:RING * G * D2].rearrange("p (r j d) -> p r j d", r=RING, j=G)
        hot = sb("hot", [P, OHR, G * P])
        assert FROWS * REC + 2 * D2 <= OHR * G * P
        fill = hot[:, :, :].rearrange("p u n -> p (u n)")[:, 0:FROWS * REC].rearrange("p (r c) -> p r c", c=REC)
        src_rest = hot[:, :, :].rearrange("p u n -> p (u n)")[:, OHR * G * P - 2 * D2:].rearrange("p (b d) -> p b d", b=2)
        attr_t = sb("attr_t", [KB, 2, G * P], BF16)
        GW = G * D2
        z = shared[:, 0:2 * GW].rearrange("p (s w) -> p s w", s=2)
        neg = shared[:, 2 * GW:4 * GW].rearrange("p (s w) -> p s w", s=2)
        parts = shared[:, 4 * GW:6 * GW].rearrange("p (s w) -> p s w", s=2)
        message = shared[:, 6 * GW:7 * GW].rearrange("p (s w) -> p s w", s=2)
        assert 7 * GW <= EP * A
        agg = sb("agg", [P, NB * D])
        assert 6 * EP <= NB * D
        eq = agg[:, 0:3 * EP // 2].bitcast(mybir.dt.int16).rearrange("p (k t) -> p k t", k=3)
        eqb = agg[:, 3 * EP // 2:3 * EP].bitcast(BF16).rearrange("p (k t) -> p k t", k=3)
        cum = agg[:, 3 * EP:6 * EP].rearrange("p (k t) -> p k t", k=3)
        BUF = (0, 1, 0, 1, 0, 1, 2)
        xs = src_parts[:, 0:2 * NB * D].bitcast(F32)
        sq = src_parts[:, 2 * NB * D:4 * NB * D].bitcast(F32)
        mean = sb("mean", [P, D])
        rstd = sb("rstd", [P, D])
        node_mean = sb("node_mean", [P, NB])
        node_rstd = sb("node_rstd", [P, NB])

        z_ps = psum("z_ps", [P, 2, GW])
        hot_ps = psum("hot_ps", [P, G * P])
        attr_ps = psum("attr_ps", [P, G * P])
        sum_ps = psum("sum_ps", [P, 2, G * D])

        def src_ps(b):
            return z_ps[:, b, 0:D2]

        def dst_ps(b):
            return z_ps[:, b, 512:512 + D2]

        def src_part(nb, k):
            return src_parts[:, bass.ds(nb * (3 * D2) + k * D2, D2)]

        S = {}

        def mk(*names):
            for n in names:
                S[n] = sem(n)
            return [S[n] for n in names]

        (src_loaded, dst_loaded, attr_loaded, weights_loaded, consts_ready, seq_done) = mk(
            "src_loaded", "dst_loaded", "attr_loaded", "weights_loaded", "consts_ready", "seq_done")
        (cleared, src_split, counted, rows_ready, base_ps, base_step) = mk(
            "cleared", "src_split", "counted", "rows_ready", "base_ps", "base_step")
        (packing, filled, taken_up, tile_blocks_ready, gb_ps, gb_ready) = mk(
            "packing", "filled", "taken_up", "tile_blocks_ready", "gb_ps", "gb_ready")
        scattered = [sem(f"scattered{i}") for i in range(2)]
        x_loaded = [sem(f"x_loaded{i}") for i in range(RING)]
        dst_stored = [sem(f"dst_stored{i}") for i in range(RING)]
        (x_turned, x_t_ready, maps_done, src_read, dst_read, rest_ready, middle_ready, low_ready) = mk(
            "x_turned", "x_t_ready", "maps_done", "src_read", "dst_read", "rest_ready", "middle_ready", "low_ready")
        (eq_done, scan_done, placed, idents_ready, w_split, w_stacked, attr_ps_ready, parts_staged) = mk(
            "eq_done", "scan_done", "placed", "idents_ready", "w_split", "w_stacked", "attr_ps_ready", "parts_staged")
        rec_loaded = [sem(f"rec_loaded{i}") for i in range(RING)]
        gathered = [sem(f"gathered{i}") for i in range(RING)]
        (hot_ready, turned, hot_t_ready, z_done, z_added, logs_ready, parts_ready, gate_ready,
         log_gate_ready, message_ready, summed, agg_added) = mk(
            "hot_ready", "turned", "hot_t_ready", "z_done", "z_added", "logs_ready", "parts_ready",
            "gate_ready", "log_gate_ready", "message_ready", "summed", "agg_added")
        (xs_loaded, col_sum, mean_ready, centered, squared, sq_sum, var_ready, std_ready, f_neg, f_log, f_y,
         f_sq, f_rstd, f_out, out_stored, nstep) = mk(
            "xs_loaded", "col_sum", "mean_ready", "centered", "squared", "sq_sum", "var_ready", "std_ready", "f_neg",
            "f_log", "f_y", "f_sq", "f_rstd", "f_out", "out_stored", "nstep")

        def after(eng, semaphore, value):
            if not isinstance(value, int) or value > 0:
                eng.wait_ge(semaphore, value)

        U = OHR

        def steps(eng, lag, step, count=GROUPS, peeled=1, between=()):
            for it in range(peeled):
                for u in range(U):
                    step(it * U, u)
                if it < len(between):
                    between[it]()
            with eng.Fori(peeled, count // U) as it:
                for u in range(U):
                    step(it * U, u)
            for u in range(count % U + lag):
                step(count - count % U, u)

        def live(base, u, lag, count=GROUPS):
            return not isinstance(base, int) or 0 <= base + u - lag < count

        def fills(base, u, lag, inc):
            return base * (inc // RING) + ((u - lag) // RING + 1) * inc

        def blocks_of(engine, g):
            word = nc.values_load(group_blocks[0:1, bass.ds(g, 1)], engines=(engine,), min_val=0, max_val=(1 << BITS * G) - 1,
                                  skip_runtime_bounds_check_because="each block was capped before they were packed")
            return [((word >> (BITS * j)) & ((1 << BITS) - 1)).with_bounds(min_val=0, max_val=NB - 1) for j in range(G)]

        block = ctx.enter_context(nc.Block())

        @block.sync
        def _(sp):
            sp.wait_ge(cleared, 1)
            sp.dma_start(src_i[0:P - 1, :], src[0:(P - 1) * EP].rearrange("(p t) -> p t", t=EP)).then_inc(src_loaded, 16)
            sp.dma_start(src_i[P - 1:P, 0:TAIL], src[(P - 1) * EP:E].rearrange("(p t) -> p t", p=1)).then_inc(src_loaded, 16)

            def load_block(base, u):
                nb, r = base + u, u % RING
                rows = LAST if isinstance(nb, int) and nb == NB - 1 else P
                after(sp, x_turned, nb - RING + 1)
                sp.dma_start(x_in[0:rows, r, :], x[bass.ds(nb * P, rows), :]).then_inc(x_loaded[r], 16)

            def store_block(base, u):
                nb, r = base + u - 6, (u - 6) % RING
                sp.wait_ge(dst_read, nb + 1)
                sp.dma_start(dst_table[bass.ds(nb * P, P), :], dst_out[:, r, :]).then_inc(dst_stored[r], 16)

            def load_rest():
                sp.wait_ge(cleared, 4)
                sp.dma_start(shared[0:P - 1, :], edge_attr[0:(P - 1) * EP, :].rearrange("(p t) a -> p (t a)", t=EP)).then_inc(attr_loaded, 16)
                sp.dma_start(shared[P - 1:P, 0:TAIL * A], edge_attr[(P - 1) * EP:E, :].rearrange("(p t) a -> p (t a)", p=1)).then_inc(attr_loaded, 16)
                sp.dma_start(dst_i[0:P - 1, :], dst[0:(P - 1) * EP].rearrange("(p t) -> p t", t=EP)).then_inc(dst_loaded, 16)
                sp.dma_start(dst_i[P - 1:P, 0:TAIL], dst[(P - 1) * EP:E].rearrange("(p t) -> p t", p=1)).then_inc(dst_loaded, 16)

            def blocks_step(base, u):
                if live(base, u, 0, NB):
                    load_block(base, u)
                if live(base, u, 6, NB):
                    store_block(base, u)

            steps(sp, 6, blocks_step, NB, 1, (load_rest,))

            sp.wait_ge(w_split, 5)
            for n, k in enumerate((0, 1, 2, 0, 1, 0)):
                sp.dma_start(w_stack[n * A:(n + 1) * A, :], w_parts[0:A, k, :]).then_inc(w_stacked, 16)
            for k in range(3):
                sp.dma_start(w_stack[K + k:K + k + 1, :], w_parts[A:A + 1, k, :]).then_inc(w_stacked, 16)

            for i in range(2):
                sp.wait_ge(scattered[i], 16 * EP // 2)
            rec_in = records[0:SPARE, :].rearrange("(g p j) c -> g p (j c)", p=P, j=G)

            def load_records(base, u):
                g, r = base + u, u % RING
                after(sp, z_added, g - RING + 1)
                sp.dma_start(rec[:, r, :, :].rearrange("p j c -> p (j c)"),
                             rec_in[bass.ds(g, 1)].rearrange("g p w -> (g p) w")).then_inc(rec_loaded[r], 16)

            steps(sp, 0, load_records)

            sp.wait_ge(z_done, GROUPS)
            sp.dma_start(xs[:, 0:(NB - 1) * D].rearrange("p (b d) -> p b d", d=D),
                         x[0:(NB - 1) * P, :].rearrange("(b p) d -> p b d", p=P)).then_inc(xs_loaded, 16)
            sp.dma_start(xs[0:LAST, (NB - 1) * D:NB * D], x[(NB - 1) * P:N, :]).then_inc(xs_loaded, 16)
            for c in range(NCH):
                sp.wait_ge(f_out, c + 1)
                b0, b1 = c * CB, min((c + 1) * CB, NB - 1)
                sp.dma_start(out[b0 * P:b1 * P, :].rearrange("(b p) d -> p b d", p=P),
                             agg[:, b0 * D:b1 * D].rearrange("p (b d) -> p b d", d=D)).then_inc(out_stored, 16)
            sp.dma_start(out[(NB - 1) * P:N, :], agg[0:LAST, (NB - 1) * D:NB * D]).then_inc(out_stored, 16)
            sp.wait_ge(out_stored, 16 * (NCH + 1))

        @block.gpsimd
        def _(pool):
            pool.iota(node_iota[:, :], pattern=[[1, P]], base=0, channel_multiplier=0,
                      allow_small_or_imprecise_dtypes=True).then_inc(consts_ready, 1)
            pool.iota(tile_iota[:, :], pattern=[[1, T]], base=0, channel_multiplier=0,
                      allow_small_or_imprecise_dtypes=True).then_inc(consts_ready, 1)
            pool.iota(pos[:, :], pattern=[[1, EP]], base=SPARE - TAIL, channel_multiplier=0,
                      allow_small_or_imprecise_dtypes=True).then_inc(consts_ready, 1)
            pool.memset(ones[:, :], 1.0).then_inc(consts_ready, 1)
            pool.memset(attr_t[:, :, :], 1.0).then_inc(consts_ready, 1)
            pool.wait_ge(consts_ready, 5)
            pool.affine_select(out=ident[:, :], in_=ones[:, :], compare_op=ALU.is_equal, fill=0.0, base=0,
                               pattern=[[-1, P]], channel_multiplier=1).then_inc(consts_ready, 1)
            pool.affine_select(out=below[:, :], in_=ones[:, :], compare_op=ALU.is_gt, fill=0.0, base=0,
                               pattern=[[1, P]], channel_multiplier=-1).then_inc(consts_ready, 1)
            pool.affine_select(out=upto[:, :], in_=ones[:, :], compare_op=ALU.is_ge, fill=0.0, base=0,
                               pattern=[[1, P]], channel_multiplier=-1).then_inc(consts_ready, 1)

            pool.wait_ge(weights_loaded, 160)
            pool.tensor_copy(w_parts[:, 0, :], w_edge[:, :]).then_inc(w_split, 1)
            pool.wait_ge(w_split, 1)
            pool.tensor_tensor(w_edge[:, :], w_edge[:, :], w_parts[:, 0, :], ALU.subtract).then_inc(w_split, 1)
            pool.wait_ge(w_split, 2)
            pool.tensor_copy(w_parts[:, 1, :], w_edge[:, :]).then_inc(w_split, 1)
            pool.wait_ge(w_split, 3)
            pool.tensor_tensor(w_edge[:, :], w_edge[:, :], w_parts[:, 1, :], ALU.subtract).then_inc(w_split, 1)
            pool.wait_ge(w_split, 4)
            pool.tensor_copy(w_parts[:, 2, :], w_edge[:, :]).then_inc(w_split, 1)

            def split_table(base, u):
                s = base + u
                if live(base, u, 2, NB):
                    pool.wait_ge(src_read, s - 1)
                    pool.tensor_tensor(src_rest[:, u % 2, :], src_rest[:, u % 2, :], src_part(s - 2, 0), ALU.subtract).then_inc(rest_ready, 1)
                if live(base, u, 3, NB):
                    pool.wait_ge(middle_ready, s - 2)
                    pool.tensor_tensor(src_part(s - 3, 2), src_rest[:, (u - 3) % 2, :], src_part(s - 3, 1), ALU.subtract).then_inc(low_ready, 1)

            steps(pool, 3, split_table, NB)

            pool.wait_ge(filled, 16 * FILL)

            with pool.Fori(0, STAGES // 2) as i:
                for h in range(2):
                    pool.wait_ge(parts_staged, i * 6 + (h * 3 + 3))
                    pool.sem_inc(taken_up, 1)
                    for c in range(CH):
                        pool.indirect_dma_start(
                            out=records, out_offset=bass.IndirectOffsetOnAxis(ap=stage_row[:, h, c:c + 1], axis=0),
                            in_=stage[:, h, c, :], in_offset=None).then_inc(scattered[h], 16)

            def gather(g, r, it):
                pool.wait_ge(rec_loaded[r], it)
                pool.sem_inc(taken_up, 1)
                for j in range(G):
                    pool.indirect_dma_start(
                        out=dst_rows[:, r, j, :], out_offset=None, in_=dst_table,
                        in_offset=bass.IndirectOffsetOnAxis(ap=rec[:, r, j, DST:DST + 1].bitcast(I32), axis=0),
                    ).then_inc(gathered[r], 16)

            for r in range(RING):
                pool.wait_ge(dst_stored[r], 16 * ((NB - r - 1) // RING + 1))

            with pool.Fori(0, GROUPS // RING) as it:
                for r in range(RING):
                    gather(it * RING + r, r, it * 16 + 16)

        @block.scalar
        def _(act):
            for k, (w, b) in enumerate(((gate_w, gate_b), (cand_w, cand_b))):
                cols = slice(k * D, (k + 1) * D)
                act.dma_start(w_src[:, cols], w[0:D, :]).then_inc(weights_loaded, 16)
                act.dma_start(w_dst[:, cols], w[D:2 * D, :]).then_inc(weights_loaded, 16)
                act.dma_start(w_edge[0:A, cols], w[2 * D:2 * D + A, :]).then_inc(weights_loaded, 16)
                act.dma_start(w_edge[A:A + 1, cols], b.rearrange("(a d) -> a d", a=1)).then_inc(weights_loaded, 16)
            act.dma_start(gamma_row[:, 0:D], gamma.rearrange("(a d) -> a d", a=1)).then_inc(weights_loaded, 16)
            act.dma_start(gamma_row[:, D:D2], beta.rearrange("(a d) -> a d", a=1)).then_inc(weights_loaded, 16)
            act.wait_ge(cleared, 2)
            rec_fill = records[0:SPARE, :].rearrange("(i p r) c -> i p (r c)", p=P, r=FROWS)
            for i in range(FILL):
                act.dma_start(rec_fill[i], fill[:, :, :].rearrange("p r c -> p (r c)")).then_inc(filled, 16)

            def evacuate(base, u):
                s = base + u
                if live(base, u, 0, NB):
                    rows = LAST if isinstance(s, int) and s == NB - 1 else P
                    b = u % 2
                    act.wait_ge(x_turned, s + 1)
                    after(act, maps_done, s - 1)
                    nc.scalar.copy(x_t[:, b, 0:rows], sum_ps[:, b, 0:rows]).then_inc(x_t_ready, 1)
                if live(base, u, 2, NB):
                    nb, b, r = s - 2, u % 2, (u - 2) % RING
                    act.wait_ge(maps_done, s - 1)
                    after(act, low_ready, s - 3)
                    nc.scalar.copy(src_rest[:, b, :], src_ps(b))
                    nc.scalar.copy(src_part(nb, 0), src_ps(b)).then_inc(src_read, 1)
                    if live(base, u, 2 + RING, NB + RING):
                        act.wait_ge(dst_stored[r], fills(base, u, 2 + RING, 16))
                    nc.scalar.copy(dst_out[:, r, :], dst_ps(b)).then_inc(dst_read, 1)
                if live(base, u, 3, NB):
                    act.wait_ge(rest_ready, s - 2)
                    nc.scalar.copy(src_part(s - 3, 1), src_rest[:, (u - 3) % 2, :]).then_inc(middle_ready, 1)

            steps(act, 3, evacuate, NB)

            act.wait_ge(dst_loaded, 32)
            stage_bf = stage[:, :, :, :].bitcast(BF16)

            def stage_columns(t0, h, i):
                after(act, scattered[h], i * (16 * CH))
                cols = bass.ds(t0, CH)

                def part(first, copies, value):
                    act.wait_ge(attr_ps_ready, value)
                    nc.scalar.copy(stage_bf[:, h, :, first * A:(first + copies) * A].rearrange("p t (k a) -> p t k a", a=A),
                                   (attr_ps, hot_ps)[h][:, 0:CH * A].rearrange("p (t a) -> p t a", a=A).unsqueeze(2)
                                   .to_broadcast([P, CH, copies, A])).then_inc(parts_staged, 1)

                part(0, 3, i * 6 + (3 * h + 1))
                nc.scalar.copy(stage[:, h, :, LO:LO + 1].rearrange("p t c -> p (t c)"), lo_f[:, cols])
                nc.scalar.copy(stage[:, h, :, DST:DST + 1].bitcast(I32).rearrange("p t c -> p (t c)"), dst_i[:, cols])
                nc.scalar.copy(stage_row[:, h, :], row_i[:, cols])
                part(3, 2, i * 6 + (3 * h + 2))
                part(5, 1, i * 6 + (3 * h + 3))

            act.wait_ge(rows_ready, 1)
            first_stages = COLS[0][1] // CH
            for k in range(first_stages):
                stage_columns(k * CH, k % 2, k // 2)
            act.wait_ge(rows_ready, 2)
            with act.Fori(first_stages // 2, STAGES // 2) as i:
                for h in range(2):
                    stage_columns(i * (2 * CH) + h * CH, h, i)

            nc.scalar.preload_act_table_set("natural_log_exp_and_others")

            def step(base, u):
                s = base + u
                b = (u - 1) % 2

                def log_part(n, to, source, function, **scaling):
                    if live(base, u, 3):
                        act.wait_ge(*((logs_ready, s * 3 + (n - 9)) if n else (z_added, s - 2)))
                        nc.scalar.activation(to[:, b, :], source[:, b, :], function, **scaling).then_inc(logs_ready, 1)

                if live(base, u, 3):
                    after(act, parts_ready, s - 4)
                log_part(0, neg, z, ACT.Abs)
                if live(base, u, 1):
                    act.wait_ge(turned, s)
                    after(act, z_done, s - 2)
                    nc.scalar.copy(hot_t[:, b, :], hot_ps[:, :])
                log_part(1, neg, neg, ACT.Exp, scale=-1.0)
                if live(base, u, 1):
                    nc.scalar.copy(attr_t[0:K, b, :], attr_ps[0:K, :]).then_inc(hot_t_ready, 1)
                log_part(2, neg, neg, ACT.Ln, bias=1.0)
                if live(base, u, 4):
                    b = (u - 4) % 2
                    act.wait_ge(log_gate_ready, s - 3)
                    gate = parts[:, b, :].rearrange("p (j d) -> p j d", d=D2)[:, :, 0:D]
                    nc.scalar.activation(gate, gate, ACT.Exp).then_inc(gate_ready, 1)

            steps(act, 4, step)

            for c in range(NCH):
                act.wait_ge(centered, c + 1)
                if c == 0:
                    act.wait_ge(col_sum, 1)
                nc.scalar.activation(sq[:, c * CW:(c + 1) * CW], agg[:, c * CW:(c + 1) * CW], ACT.Square).then_inc(squared, 1)
            act.wait_ge(var_ready, 1)
            nc.scalar.activation(rstd[:, :], rstd[:, :], ACT.Sqrt).then_inc(std_ready, 1)
            nc.scalar.preload_act_table_set("natural_log_exp_and_others")
            for c in range(NCH):
                part = sq[:, c * CW:(c + 1) * CW]
                act.wait_ge(f_neg, c + 1)
                nc.scalar.activation(part, part, ACT.Exp).then_inc(f_log, 1)
                act.wait_ge(f_log, 2 * c + 1)
                nc.scalar.activation(part, part, ACT.Ln, bias=1.0).then_inc(f_log, 1)
            for c in range(NCH):
                part = sq[:, c * CW:(c + 1) * CW]
                act.wait_ge(f_y, c + 1)
                nc.scalar.activation(part, agg[:, c * CW:(c + 1) * CW], ACT.Square).then_inc(f_sq, 1)
            act.wait_ge(f_rstd, 1)
            nc.scalar.activation(node_rstd[:, :], node_rstd[:, :], ACT.Sqrt).then_inc(f_rstd, 1)

        @block.vector
        def _(dve):
            v = nc.vector
            v.memset(src_i[:, :], NB * P).then_inc(cleared, 1)
            v.memset(fill[:, :, :], 0.0).then_inc(nstep, 1)
            dve.wait_ge(nstep, 1)
            v.memset(fill[:, :, LO:LO + 1], -1.0).then_inc(cleared, 1)
            v.memset(dst_i[96:P, TAIL:EP], 0).then_inc(cleared, 1)
            v.memset(shared[96:P, TAIL * A:EP * A], 0.0).then_inc(cleared, 1)

            dve.wait_ge(src_loaded, 32)
            v.tensor_scalar(lo_i[:, :], src_i[:, :], P - 1, None, ALU.bitwise_and).then_inc(src_split, 1)
            v.tensor_scalar(row_i[:, :], src_i[:, :], 7, None, ALU.logical_shift_right).then_inc(src_split, 1)
            dve.wait_ge(src_split, 2)
            v.tensor_copy(lo_f[:, :], lo_i[:, :]).then_inc(src_split, 1)
            v.tensor_copy(hi_f[:, :], row_i[:, :]).then_inc(src_split, 1)
            dve.wait_ge(src_split, 4)
            dve.wait_ge(consts_ready, 8)
            v.tensor_copy(ident_bf[:, :], ident[:, :]).then_inc(idents_ready, 1)
            v.tensor_scalar(minus_ident[:, :], ident[:, :], -1.0, None, ALU.mult).then_inc(idents_ready, 1)

            def count_seven(b0):
                for k in range(7):
                    b = b0 + k
                    after(dve, counted, b - 1 if k else b)
                    v.tensor_scalar(eqb[:, BUF[k], :], hi_f[:, :], node_iota[:, bass.ds(b, 1)], 0.0, ALU.is_equal, ALU.add,
                                    accum_out=count[:, bass.ds(b, 1)]).then_inc(counted, 1)

            count_seven(0)
            with dve.Fori(1, NB // 7) as i:
                count_seven(i * 7)
            dve.wait_ge(base_ps, 1)
            v.tensor_scalar(total_f[:, :], attr_ps[0:NB, NB:NB + 1], float(P - 1), None, ALU.add).then_inc(base_step, 1)
            dve.wait_ge(base_step, 1)
            v.tensor_copy(total_i[:, :], total_f[:, :]).then_inc(base_step, 1)
            dve.wait_ge(base_step, 2)
            v.tensor_scalar(total_i[:, :], total_i[:, :], 7, None, ALU.logical_shift_right).then_inc(base_step, 1)
            dve.wait_ge(base_step, 3)
            v.tensor_copy(block_tiles[:, :], total_i[:, :]).then_inc(base_step, 1)
            dve.wait_ge(base_step, 4)
            v.tensor_scalar(tiles_below[:, :], below[0:NB, 0:NB], block_tiles[:, 0:1], None, ALU.mult).then_inc(base_step, 1)
            dve.wait_ge(base_ps, 2)
            v.tensor_scalar(first[:, :], attr_ps[:, 256:256 + NB], float(P), -1.0, ALU.mult, ALU.add).then_inc(base_step, 1)
            v.tensor_copy(block_end[:, :], attr_ps[0:NB, 256 + NB:257 + NB]).then_inc(base_step, 1)
            dve.wait_ge(base_step, 7)
            v.tensor_tensor(first[:, :], first[:, :], attr_ps[:, 0:NB], ALU.add).then_inc(base_step, 1)
            v.tensor_scalar(begun[:, :], tile_iota[:, :], block_end[:, 0:1], None, ALU.is_ge).then_inc(base_step, 1)
            dve.wait_ge(base_step, 9)

            for n, (t0, t1) in enumerate(COLS):
                w = t1 - t0

                def equal(b, k):
                    v.tensor_scalar(eq[:, k, t0:t1], hi_f[:, t0:t1], node_iota[:, bass.ds(b, 1)], None,
                                    ALU.is_equal).then_inc(eq_done, 1)

                def place_seven(b0):
                    for k in range(7):
                        b, m = b0 + k, BUF[k]
                        dve.wait_ge(eq_done, b + (n * (NB + 1) + 1))
                        v.tensor_tensor_scan(cum[:, m, t0:t1], eq[:, m, t0:t1], eq[:, m, t0:t1], first[:, bass.ds(b, 1)],
                                             ALU.add, ALU.bypass).then_inc(scan_done, 1)
                        after(dve, placed, b + n * NB)
                        equal(b + 1, BUF[(k + 1) % 7])
                        dve.wait_ge(scan_done, b + (n * NB + 1))
                        v.tensor_scalar(first[:, bass.ds(b, 1)], cum[:, m, t1 - 1:t1], 0.0, None, ALU.add)
                        v.copy_predicated(pos[:, t0:t1], eq[:, m, t0:t1], cum[:, m, t0:t1]).then_inc(placed, 1)

                equal(0, 0)
                if n == 0:
                    place_seven(0)
                with dve.Fori(1 - n, NB // 7) as i:
                    place_seven(i * 7)
                dve.wait_ge(placed, (n + 1) * NB)
                done = n * 6 - 1
                v.tensor_copy(row_i[:, t0:t1], pos[:, t0:t1]).then_inc(nstep, 1)
                dve.wait_ge(nstep, done + 3)
                v.tensor_scalar(src_i[:, t0:t1], row_i[:, t0:t1], P - 1, GH, ALU.bitwise_and, ALU.logical_shift_left).then_inc(nstep, 1)
                v.tensor_scalar(lo_i[:, t0:t1], row_i[:, t0:t1], 7, G - 1, ALU.logical_shift_right, ALU.bitwise_and).then_inc(nstep, 1)
                v.tensor_scalar(row_i[:, t0:t1], row_i[:, t0:t1], 7 + GH, 7 + GH, ALU.logical_shift_right, ALU.logical_shift_left).then_inc(nstep, 1)
                dve.wait_ge(nstep, done + 6)
                v.tensor_tensor(row_i[:, t0:t1], row_i[:, t0:t1], src_i[:, t0:t1], ALU.bitwise_or).then_inc(nstep, 1)
                dve.wait_ge(nstep, done + 7)
                v.tensor_tensor(row_i[:, t0:t1], row_i[:, t0:t1], lo_i[:, t0:t1], ALU.bitwise_or).then_inc(nstep, 1)
                dve.wait_ge(nstep, done + 8)
                dve.sem_inc(rows_ready, 1)
                if n == 1:
                    v.memset(agg[:, :], 0.0).then_inc(nstep, 1)
                    dve.wait_ge(base_ps, 3)
                    v.tensor_scalar(tile_block[:, :, :].rearrange("p (k g) j -> p k (g j)", k=2), sum_ps[0:1, :, 0:T // 2], float(NB - 1),
                                    None, ALU.min).then_inc(packing, 1)
                    acc = tile_block[:, :, G - 1]
                    for k, j in enumerate(range(G - 2, -1, -1)):
                        dve.wait_ge(packing, k + 1)
                        v.scalar_tensor_tensor(out=packed[:, :], in0=acc, scalar=float(1 << BITS), in1=tile_block[:, :, j],
                                               op0=ALU.mult, op1=ALU.add).then_inc(packing, 1)
                        acc = packed[:, :]
                    dve.wait_ge(packing, G)
                    v.tensor_copy(group_blocks[:, :], packed[:, :]).then_inc(tile_blocks_ready, 1)
                    dve.wait_ge(gb_ps, 1)
                    v.tensor_copy(gb[:, :], sum_ps[:, 0, 0:D2]).then_inc(gb_ready, 1)

            def step(base, u):
                s = base + u
                if live(base, u, 7):
                    at = blocks_of(mybir.EngineType.DVE, s - 7)

                def add_sum(j):
                    if live(base, u, 7):
                        if j == 0:
                            dve.wait_ge(summed, s - 6)
                        else:
                            dve.wait_ge(agg_added, (s - 7) * G + j)
                        part = agg[:, bass.ds(at[j] * D, D)]
                        v.tensor_tensor(part, part, sum_ps[:, (u - 7) % 2, j * D:(j + 1) * D], ALU.add).then_inc(agg_added, 1)

                if live(base, u, 3):
                    r, b = (u - 3) % RING, (u - 3) % 2
                    dve.wait_ge(gathered[r], fills(base, u, 3, 16 * G))
                    dve.wait_ge(z_done, s - 2)
                    after(dve, parts_ready, s - 4)
                    v.tensor_tensor(z[:, b, :], z_ps[:, b, :], dst_rows[:, r, :, :].rearrange("p j d -> p (j d)"),
                                    ALU.add).then_inc(z_added, 1)
                if live(base, u, 7):
                    after(dve, agg_added, (s - 7) * G)
                add_sum(0)
                if live(base, u, 0):
                    r = u % RING
                    dve.wait_ge(rec_loaded[r], fills(base, u, 0, 16))
                    after(dve, summed, s - OHR + 1)
                    v.tensor_tensor(hot[:, u, :].rearrange("p (j n) -> p j n", n=P),
                                    node_iota[:, :].unsqueeze(1).to_broadcast([P, G, P]),
                                    rec[:, r, :, LO:LO + 1].to_broadcast([P, G, P]), ALU.is_equal).then_inc(hot_ready, 1)
                add_sum(1)
                if live(base, u, 4):
                    b = (u - 4) % 2

                    def half(a, k):
                        return a[:, b, :].rearrange("p (j d) -> p j d", d=D2)[:, :, k * D:(k + 1) * D]

                    dve.wait_ge(logs_ready, s * 3 - 9)
                    after(dve, message_ready, s - 5)
                    v.scalar_tensor_tensor(out=half(parts, 0), in0=half(z, 0), scalar=0.0, in1=half(neg, 0), op0=ALU.min,
                                           op1=ALU.subtract).then_inc(log_gate_ready, 1)
                    v.scalar_tensor_tensor(out=half(parts, 1), in0=half(z, 1), scalar=0.0, in1=half(neg, 1), op0=ALU.max,
                                           op1=ALU.add).then_inc(parts_ready, 1)
                add_sum(2)
                if live(base, u, 5):
                    b = (u - 5) % 2
                    dve.wait_ge(gate_ready, s - 4)
                    after(dve, summed, s - 6)
                    halves = parts[:, b, :].rearrange("p (j d) -> p j d", d=D2)
                    v.tensor_tensor(message[:, b, :].rearrange("p (j d) -> p j d", d=D), halves[:, :, 0:D],
                                    halves[:, :, D:D2], ALU.mult).then_inc(message_ready, 1)
                add_sum(3)

            steps(dve, 7, step)

            dve.wait_ge(agg_added, T)
            base = 14
            dve.wait_ge(col_sum, 1)
            v.tensor_reduce(mean[:, :], sum_ps[:, 0, :].rearrange("p (c f) -> p f c", f=D), AX_X, ALU.add).then_inc(nstep, 1)
            dve.wait_ge(nstep, base + 1)
            v.tensor_scalar(mean[:, :], mean[:, :], 1.0 / N, None, ALU.mult).then_inc(mean_ready, 1)
            dve.wait_ge(mean_ready, 1)

            def blocks(a, c, w=CB):
                return a[:, c * CW:(c + 1) * CW].rearrange("p (b d) -> p b d", d=D)

            def every_block(a):
                return a.unsqueeze(1).to_broadcast([P, CB, D])

            for c in range(NCH):
                v.tensor_tensor(blocks(agg, c), blocks(agg, c), every_block(mean[:, :]), ALU.subtract).then_inc(centered, 1)
            dve.wait_ge(sq_sum, 1)
            v.tensor_reduce(rstd[:, :], sum_ps[:, 1, :].rearrange("p (c f) -> p f c", f=D), AX_X, ALU.add).then_inc(nstep, 1)
            dve.wait_ge(nstep, base + 2)
            v.tensor_scalar(rstd[:, :], rstd[:, :], 1.0 / N, BN_EPS, ALU.mult, ALU.add).then_inc(var_ready, 1)
            dve.wait_ge(std_ready, 1)
            v.reciprocal(rstd[:, :], rstd[:, :]).then_inc(nstep, 1)
            dve.wait_ge(nstep, base + 3)
            dve.wait_ge(gb_ready, 1)
            v.tensor_tensor(rstd[:, :], rstd[:, :], gb[:, 0:D], ALU.mult).then_inc(nstep, 1)
            dve.wait_ge(nstep, base + 4)
            dve.wait_ge(xs_loaded, 32)
            dve.wait_ge(squared, NCH)
            n = base + 4
            for c in range(NCH):
                a, xb = blocks(agg, c), blocks(xs, c)
                v.tensor_tensor(a, a, every_block(rstd[:, :]), ALU.mult).then_inc(nstep, 1)
                n += 1
                dve.wait_ge(nstep, n)
                v.tensor_tensor(a, a, every_block(gb[:, D:D2]), ALU.add).then_inc(nstep, 1)
                n += 1
                dve.wait_ge(nstep, n)
                v.tensor_tensor(a, a, xb, ALU.add).then_inc(nstep, 1)
                n += 1
                dve.wait_ge(nstep, n)
                t = agg[:, c * CW:(c + 1) * CW]
                v.scalar_tensor_tensor(out=sq[:, c * CW:(c + 1) * CW], in0=t, scalar=-1.0, in1=t, op0=ALU.mult,
                                       op1=ALU.min).then_inc(f_neg, 1)
            for c in range(NCH):
                a, xb, l = blocks(agg, c), blocks(xs, c), blocks(sq, c)
                mb = node_mean[:, c * CB:(c + 1) * CB]
                dve.wait_ge(f_log, 2 * c + 2)
                v.scalar_tensor_tensor(out=a, in0=a, scalar=0.0, in1=l, op0=ALU.max, op1=ALU.add).then_inc(nstep, 1)
                n += 1
                dve.wait_ge(nstep, n)
                v.tensor_tensor(a, a, xb, ALU.add).then_inc(nstep, 1)
                n += 1
                dve.wait_ge(nstep, n)
                v.tensor_reduce(mb, a, AX_X, ALU.add).then_inc(nstep, 1)
                n += 1
                dve.wait_ge(nstep, n)
                v.tensor_scalar(mb, mb, 1.0 / D, None, ALU.mult).then_inc(nstep, 1)
                n += 1
                dve.wait_ge(nstep, n)
                v.tensor_tensor(a, a, mb.unsqueeze(2).to_broadcast([P, CB, D]), ALU.subtract).then_inc(f_y, 1)
            for c in range(NCH):
                dve.wait_ge(f_sq, c + 1)
                v.tensor_reduce(node_rstd[:, c * CB:(c + 1) * CB], blocks(sq, c), AX_X, ALU.add).then_inc(nstep, 1)
                n += 1
            dve.wait_ge(nstep, n)
            v.tensor_scalar(node_rstd[:, :], node_rstd[:, :], 1.0 / D, LN_EPS, ALU.mult, ALU.add).then_inc(f_rstd, 1)
            dve.wait_ge(f_rstd, 2)
            v.reciprocal(node_rstd[:, :], node_rstd[:, :]).then_inc(nstep, 1)
            n += 1
            dve.wait_ge(nstep, n)
            for c in range(NCH):
                rb = node_rstd[:, c * CB:(c + 1) * CB]
                v.tensor_tensor(blocks(agg, c), blocks(agg, c), rb.unsqueeze(2).to_broadcast([P, CB, D]),
                                ALU.mult).then_inc(f_out, 1)

        @block.tensor
        def _(pe):
            def tables(base, u):
                s = base + u
                if live(base, u, 0, NB):
                    r, b = u % RING, u % 2
                    rows = LAST if isinstance(s, int) and s == NB - 1 else P
                    pe.wait_ge(x_loaded[r], fills(base, u, 0, 16))
                    after(pe, x_t_ready, s - 1)
                    pe.transpose(sum_ps[:, b, 0:rows], x_in[0:rows, r, :], ident[0:rows, 0:rows]).then_inc(x_turned, 1)
                if live(base, u, 1, NB):
                    b = (u - 1) % 2
                    pe.wait_ge(x_t_ready, s)
                    after(pe, src_read, s - 2)
                    after(pe, dst_read, s - 2)
                    pe.matmul(src_ps(b), x_t[:, b, :], w_src[:, :], start=True, stop=True)
                    pe.matmul(dst_ps(b), x_t[:, b, :], w_dst[:, :], start=True, stop=True).then_inc(maps_done, 1)

            def edges_before():
                pe.wait_ge(counted, NB)
                pe.matmul(attr_ps[:, 0:NB], below[:, :], count[:, :], start=True, stop=True)
                pe.matmul(attr_ps[0:NB, NB:NB + 1], count[:, :], ones[:, 0:1], start=True, stop=True).then_inc(base_ps, 1)

            def tiles_before():
                pe.wait_ge(base_step, 5)
                pe.matmul(attr_ps[:, 256:256 + NB], ones[0:NB, :], tiles_below[:, :], start=True, stop=True)
                pe.matmul(attr_ps[0:NB, 256 + NB:257 + NB], upto[0:NB, 0:NB], block_tiles[:, :], start=True, stop=True).then_inc(base_ps, 1)

            def prefixes():
                edges_before()
                tiles_before()

            pe.wait_ge(consts_ready, 8)
            pe.wait_ge(idents_ready, 2)
            pe.wait_ge(weights_loaded, 160)
            steps(pe, 1, tables, NB, 2, (lambda: None, prefixes))

            pe.wait_ge(base_step, 9)
            pe.wait_ge(x_t_ready, NB)
            for k in range(2):
                mm = pe.matmul(sum_ps[0:1, k, 0:T // 2], ones[0:NB, 0:1], begun[:, k * (T // 2):(k + 1) * (T // 2)],
                               start=True, stop=True)
            mm.then_inc(base_ps, 1)

            stage_bf = stage[:, :, :, :].bitcast(BF16)

            def split_columns(h, i):
                to = (attr_ps, hot_ps)[h][:, 0:CH * A]
                for k in range(3):
                    if k:
                        pe.wait_ge(parts_staged, i * 6 + (h * 3 + k))
                    else:
                        after(pe, parts_staged, i * 6 + (h * 3 - 3))
                    mm = pe.matmul(to, ident[:, :], shared[:, bass.ds(i * (2 * CH * A) + h * CH * A, CH * A)], start=True,
                                   stop=k == 0)
                    for n in range(k):
                        mm = pe.matmul(to, minus_ident[:, :], stage_bf[:, h, :, 3 * n * A:(3 * n + 1) * A], start=False,
                                       stop=n == k - 1)
                    mm.then_inc(attr_ps_ready, 1)

            pe.wait_ge(attr_loaded, 32)
            for h in range(2):
                split_columns(h, 0)
            with pe.Fori(1, STAGES // 2) as i:
                for h in range(2):
                    split_columns(h, i)

            pe.wait_ge(tile_blocks_ready, 1)
            pe.matmul(sum_ps[:, 0, 0:D2], ones[0:1, :], gamma_row[:, :], start=True, stop=True).then_inc(gb_ps, 1)
            pe.wait_ge(gb_ready, 1)
            pe.wait_ge(low_ready, NB)
            pe.wait_ge(w_stacked, 144)

            def step(base, u):
                s = base + u
                if live(base, u, 2):
                    at = blocks_of(mybir.EngineType.PE, s - 2)
                if live(base, u, 1):
                    pe.wait_ge(hot_ready, s)
                    after(pe, hot_t_ready, s - 1)
                    for j in range(G):
                        pe.transpose(hot_ps[:, j * P:(j + 1) * P], hot[:, (u - 1) % OHR, j * P:(j + 1) * P], ident[:, :])
                        mm = pe.matmul(attr_ps[0:K, j * P:(j + 1) * P], rec[:, (u - 1) % RING, j, 0:LO].bitcast(BF16), ident_bf[:, :],
                                       start=True, stop=True)
                    mm.then_inc(turned, 1)
                if live(base, u, 2):
                    b = (u - 2) % 2
                    pe.wait_ge(hot_t_ready, s - 1)
                    after(pe, z_added, s - 3)
                    for j in range(G):
                        to = z_ps[:, b, j * D2:(j + 1) * D2]
                        pe.matmul(to, attr_t[:, b, j * P:(j + 1) * P], w_stack[:, :], start=True, stop=False)
                        for k in range(3):
                            mm = pe.matmul(to, hot_t[:, b, j * P:(j + 1) * P],
                                           src_parts[:, bass.ds(at[j] * (3 * D2) + k * D2, D2)], start=False, stop=k == 2)
                    mm.then_inc(z_done, 1)
                if live(base, u, 6):
                    pe.wait_ge(message_ready, s - 5)
                    after(pe, agg_added, (s - 7) * G)
                    o, b = (u - 6) % OHR, (u - 6) % 2
                    for j in range(G):
                        mm = pe.matmul(sum_ps[:, b, j * D:(j + 1) * D], hot[:, o, j * P:(j + 1) * P],
                                       message[:, b, j * D:(j + 1) * D], start=True, stop=True)
                    mm.then_inc(summed, 1)

            steps(pe, 6, step)

            def node_sums(a, to):
                full = (NB - 1) // G
                for c in range(full):
                    pe.matmul(to, ones[:, :], a[:, c * G * D:(c + 1) * G * D], start=(c == 0), stop=False)
                assert NB - 1 == full * G
                return pe.matmul(to[:, 0:D], ones[0:LAST, :], a[0:LAST, (NB - 1) * D:NB * D], start=False, stop=True)

            pe.wait_ge(agg_added, T)
            node_sums(agg, sum_ps[:, 0, :]).then_inc(col_sum, 1)
            pe.wait_ge(squared, NCH)
            node_sums(sq, sum_ps[:, 1, :]).then_inc(sq_sum, 1)


_INS = ['x', 'src', 'dst', 'edge_attr_10', 'L0_gnn_gate_w', 'L0_gnn_gate_b', 'L0_gnn_cand_w', 'L0_gnn_cand_b',
        'L0_gnn_bn_gamma', 'L0_gnn_bn_beta']


def kernel(**inputs):
    import numpy as _np
    import concourse.bacc as _bacc
    from concourse import mybir as _mybir
    from concourse.bass_utils import run_bass_kernel_spmd as _run

    nc = _bacc.Bacc("TRN2", target_bir_lowering=False, num_devices=1)
    arrays, args = {}, []
    for name in _INS:
        a = _np.ascontiguousarray(inputs[name])
        arrays[f"in_{name}_dram"] = a
        args.append(nc.dram_tensor(f"in_{name}_dram", a.shape, _mybir.dt.from_np(a.dtype), kind="ExternalInput").ap())
    shape = tuple(inputs['x'].shape)
    args.append(nc.dram_tensor("out_0_dram", shape, _mybir.dt.float32, kind="ExternalOutput").ap())
    gnn_kernel(nc, *args)
    r = _run(nc, [arrays], core_ids=[0])
    return r.results[0]["out_0_dram"]
```

```python
from contextlib import ExitStack

import concourse.bass as bass
from concourse import mybir

P = 128
ALU = mybir.AluOpType
ACT = mybir.ActivationFunctionType
F32 = mybir.dt.float32
BF16 = mybir.dt.bfloat16
I32 = mybir.dt.int32
AX_X = mybir.AxisListType.X

BN_EPS = 1e-5
LN_EPS = 1e-5


def gnn_kernel(nc, x, src, dst, edge_attr, gate_w, gate_b, cand_w, cand_b, gamma, beta, out):
    N, D = x.shape
    E, A = edge_attr.shape
    D2 = 2 * D
    NB = -(-N // P)
    LAST = N - (NB - 1) * P
    assert D == P and NB % 2 == 1 and NB % 7 == 0

    CH = 17
    EP = -(-E // (P * 2 * CH)) * 2 * CH
    TAIL = E - (P - 1) * EP
    assert 0 < TAIL <= EP
    STAGES = EP // CH
    STAGES1 = 8
    PIECES = [0, 2, STAGES1 + 2, STAGES]
    EARLY = NB - (STAGES - STAGES1)
    assert STAGES % 2 == 0 and STAGES1 % 2 == 0 and EARLY >= 4

    K = 6 * A
    LO = K
    KR = K + 4
    DST = KR // 2 - 1
    REC = KR // 2
    assert 2 * KR == P and N < 1 << 14
    G = 4
    RING = 4
    OHR = 8
    tiles = (E + NB * (P - 1)) // P
    GROUPS = -(-tiles // (G * OHR)) * OHR
    T = GROUPS * G
    GROWS = G * P
    SPARE = T * P
    assert EP - TAIL <= P
    GH = G.bit_length() - 1
    FILL = 8
    FROWS = T // FILL

    NCH = 7
    CB = NB // NCH
    CW = CB * D
    PE_BLOCKS = 16
    PE_SQUARES = 24
    LN_LAG = 5
    ACT_OUT = 5

    with ExitStack() as ctx:
        def sb(name, shape, dt=F32):
            return ctx.enter_context(nc.sbuf_tensor(name, shape, dt))

        def psum(name, shape, dt=F32):
            return ctx.enter_context(nc.psum_tensor(name, shape, dt))

        def sem(name):
            return ctx.enter_context(nc.semaphore(name))

        records = nc.dram_tensor("records", [SPARE + GROWS * P // G, REC], F32, kind="Internal").ap()
        dst_table = nc.dram_tensor("dst_table", [NB * P, D2], F32, kind="Internal").ap()

        ident = sb("ident", [P, P])
        below = sb("below", [P, P])
        upto = sb("upto", [P, P])
        ones = sb("ones", [P, P])
        node_iota = sb("node_iota", [P, P])
        tile_iota = sb("tile_iota", [NB, T])
        w_src = sb("w_src", [P, D2])
        w_dst = sb("w_dst", [P, D2])
        w_edge = sb("w_edge", [A, D2])
        bias_row = sb("bias_row", [1, D2])
        w_parts = sb("w_parts", [A, 3, D2], BF16)
        w_stack = sb("w_stack", [P, 2, D2], BF16)
        ident_bf = sb("ident_bf", [P, P], BF16)
        minus_ident = sb("minus_ident", [P, P], BF16)
        gamma_row = sb("gamma_row", [1, D2])
        gb = sb("gb", [P, D2])
        ranking = sb("ranking", [P, 6 * EP])
        def rank_buf(k, dt=F32):
            return ranking[:, k * EP:(k + 1) * EP] if dt is F32 else ranking[:, k * EP:(k + 1) * EP].bitcast(dt)

        src_i, dst_i, lo_i, row_i = (rank_buf(k, I32) for k in range(4))
        lo_f, pos = (rank_buf(k) for k in (4, 5))
        hi_f = sb("hi_f", [P, EP], BF16)
        count = sb("count", [P, NB])
        first = sb("first", [P, NB])
        total_f = sb("total_f", [NB, 1])
        total_i = sb("total_i", [NB, 1], I32)
        block_tiles = sb("block_tiles", [NB, 1])
        block_end = sb("block_end", [NB, 1])
        tiles_below = sb("tiles_below", [NB, NB])
        begun = sb("begun", [NB, T])
        tile_block = sb("tile_block", [1, GROUPS, G])
        LAST_Z = slice((G - 1) * D2, G * D2)
        BITS = (NB - 1).bit_length()
        assert BITS * G <= 24
        packed = sb("packed", [1, GROUPS])
        group_blocks = sb("group_blocks", [1, GROUPS], I32)
        stage = sb("stage", [P, 2, CH, REC])
        stage_bf = stage[:, :, :, :].bitcast(BF16)
        stage_row = sb("stage_row", [P, 2, CH], I32)
        x_in = sb("x_in", [P, RING, D])
        x_t = sb("x_t", [P, 2, D])
        src_parts = sb("src_parts", [P, NB * 3 * D2], BF16)
        dst_out = sb("dst_out", [P, RING, D2])
        shared = sb("shared", [P, EP * A])
        attr = shared[:, :].rearrange("p (t a) -> p t a", a=A)
        rec = sb("rec", [P, RING, G, REC])
        rec_bf = rec[:, :, :, :].bitcast(BF16)
        assert RING * G * D2 + G * P <= 6 * EP
        hot_t = ranking[:, 6 * EP - G * P:].bitcast(BF16).rearrange("p (b n) -> p b n", b=2)
        dst_rows = ranking[:, 0:RING * G * D2].rearrange("p (r j d) -> p r j d", r=RING, j=G)
        hot = sb("hot", [P, OHR, G * P])
        assert FROWS * REC + 2 * D2 <= OHR * G * P
        fill = hot[:, :, :].rearrange("p u n -> p (u n)")[:, 0:FROWS * REC].rearrange("p (r c) -> p r c", c=REC)
        src_rest = hot[:, :, :].rearrange("p u n -> p (u n)")[:, OHR * G * P - 2 * D2:].rearrange("p (b d) -> p b d", b=2)
        attr_t = sb("attr_t", [P, 2, G // 2 * P], BF16)
        GW = G * D2
        z = shared[:, 0:2 * GW].rearrange("p (s w) -> p s w", s=2)
        neg = shared[:, 2 * GW:4 * GW].rearrange("p (s w) -> p s w", s=2)
        parts = shared[:, 4 * GW:6 * GW].rearrange("p (s w) -> p s w", s=2)
        message = shared[:, 6 * GW:7 * GW].rearrange("p (s w) -> p s w", s=2)
        assert 7 * GW <= EP * A
        agg = sb("agg", [P, NB * D])
        assert 6 * EP <= NB * D
        eq = agg[:, 0:3 * EP // 2].bitcast(mybir.dt.int16).rearrange("p (k t) -> p k t", k=3)
        eqb = agg[:, 3 * EP // 2:3 * EP].bitcast(BF16).rearrange("p (k t) -> p k t", k=3)
        cum = agg[:, 3 * EP:6 * EP].rearrange("p (k t) -> p k t", k=3)
        BUF = (0, 1, 0, 1, 0, 1, 2)
        xs = src_parts[:, 0:2 * NB * D].bitcast(F32)
        sq = src_parts[:, 2 * NB * D:4 * NB * D].bitcast(F32)
        x_beta = src_parts[:, 4 * NB * D:6 * NB * D].bitcast(F32)
        mean = sb("mean", [P, D])
        rstd = sb("rstd", [P, D])
        node_scratch = hot[:, :, :].rearrange("p u n -> p (u n)")
        node_stats = node_scratch[:, 0:NB * 6].rearrange("p (b s) -> p b s", s=6)
        node_mv = node_scratch[:, NB * 6:NB * 8].rearrange("p (b s) -> p b s", s=2)
        node_rstd = node_scratch[:, NB * 8:NB * 9]
        node_shift = node_scratch[:, NB * 9:NB * 10]
        node_var = node_scratch[:, NB * 10:NB * 11]
        node_newton = node_scratch[:, NB * 11:NB * 12]
        var = node_scratch[:, NB * 12:NB * 12 + D]
        newton = node_scratch[:, NB * 12 + D:NB * 12 + 2 * D]

        z_ps = psum("z_ps", [P, 2, GW])
        hot_ps = psum("hot_ps", [P, G * P])
        attr_ps = psum("attr_ps", [P, G * P])
        sum_ps = psum("sum_ps", [P, 2, G * D])

        def src_ps(b):
            return z_ps[:, b, 0:D2]

        def dst_ps(b):
            return z_ps[:, b, 512:512 + D2]

        def src_part(nb, k):
            return src_parts[:, bass.ds(nb * (3 * D2) + k * D2, D2)]

        S = {}

        def mk(*names):
            for n in names:
                S[n] = sem(n)
            return [S[n] for n in names]

        (src_loaded, dst_loaded, attr_loaded, weights_loaded, consts_ready, gate_turned) = mk(
            "src_loaded", "dst_loaded", "attr_loaded", "weights_loaded", "consts_ready", "gate_turned")
        (cleared, src_split, counted, rows_ready, base_ps, base_step) = mk(
            "cleared", "src_split", "counted", "rows_ready", "base_ps", "base_step")
        (packing, filled, taken_up, tile_blocks_ready, gb_ps, gb_ready) = mk(
            "packing", "filled", "taken_up", "tile_blocks_ready", "gb_ps", "gb_ready")
        scattered = [sem(f"scattered{i}") for i in range(2)]
        x_loaded = [sem(f"x_loaded{i}") for i in range(RING)]
        dst_stored = [sem(f"dst_stored{i}") for i in range(RING)]
        late_x_loaded = [sem(f"late_x_loaded{i}") for i in range(2)]
        late_dst_stored = [sem(f"late_dst_stored{i}") for i in range(2)]
        (x_turned, x_t_ready, maps_done, src_read, dst_read, rest_ready, middle_ready, low_ready) = mk(
            "x_turned", "x_t_ready", "maps_done", "src_read", "dst_read", "rest_ready", "middle_ready", "low_ready")
        (eq_done, scan_done, placed, idents_ready, w_cleared, w_split, w_stacked, attr_ps_ready, parts_staged) = mk(
            "eq_done", "scan_done", "placed", "idents_ready", "w_cleared", "w_split", "w_stacked", "attr_ps_ready", "parts_staged")
        rec_loaded = [sem(f"rec_loaded{i}") for i in range(RING)]
        gathered = [sem(f"gathered{i}") for i in range(RING)]
        (hot_ready, turned, hot_t_ready, z_done, z_full, last_z_copied, z_added, logs_ready, parts_ready, gate_ready,
         message_ready, summed, agg_added) = mk(
            "hot_ready", "turned", "hot_t_ready", "z_done", "z_full", "last_z_copied", "z_added", "logs_ready", "parts_ready",
            "gate_ready", "message_ready", "summed", "agg_added")
        (xs_loaded, x_beta_ready, part_sum, col_sum, mean_ready, centered, squared, part_sq, sq_sum, var_ready,
         rstd_ready, t_ready, f_abs, f_exp, f_log, softplus_x, y_ready, stats_ready, mv_ready, f_rstd, f_shift,
         newton_done, node_newton_done, node_product, var_sum, scaled, f_out, act_out, out_stored, nstep) = mk(
            "xs_loaded", "x_beta_ready", "part_sum", "col_sum", "mean_ready", "centered", "squared", "part_sq", "sq_sum",
            "var_ready", "rstd_ready", "t_ready", "f_abs", "f_exp", "f_log", "softplus_x", "y_ready", "stats_ready",
            "mv_ready", "f_rstd", "f_shift", "newton_done", "node_newton_done", "node_product", "var_sum", "scaled",
            "f_out", "act_out", "out_stored", "nstep")

        def newton_step(eng, engine, r, v, q, done, count):
            engine.tensor_tensor(q, v, r, ALU.mult).then_inc(done, 1)
            eng.wait_ge(done, count + 1)
            engine.tensor_tensor(q, q, r, ALU.mult).then_inc(done, 1)
            eng.wait_ge(done, count + 2)
            engine.tensor_scalar(q, q, -0.5, 1.5, ALU.mult, ALU.add).then_inc(done, 1)
            eng.wait_ge(done, count + 3)
            engine.tensor_tensor(r, r, q, ALU.mult).then_inc(done, 1)
            eng.wait_ge(done, count + 4)

        def after(eng, semaphore, value):
            if not isinstance(value, int) or value > 0:
                eng.wait_ge(semaphore, value)

        U = OHR

        def steps(eng, lag, step, count=GROUPS):
            for u in range(U):
                step(0, u)
            if count // U > 1:
                with eng.Fori(1, count // U) as it:
                    for u in range(U):
                        step(it * U, u)
            for u in range(count % U + lag):
                step(count - count % U, u)

        def live(base, u, lag, count=GROUPS):
            return not isinstance(base, int) or 0 <= base + u - lag < count

        def fills(base, u, lag, inc):
            return base * (inc // RING) + ((u - lag) // RING + 1) * inc

        def blocks_of(engine, g):
            word = nc.values_load(group_blocks[0:1, bass.ds(g, 1)], engines=(engine,), min_val=0, max_val=(1 << BITS * G) - 1,
                                  skip_runtime_bounds_check_because="each block was capped before they were packed")
            return [((word >> (BITS * j)) & ((1 << BITS) - 1)).with_bounds(min_val=0, max_val=NB - 1) for j in range(G)]

        block = ctx.enter_context(nc.Block())

        @block.sync
        def _(sp):
            sp.wait_ge(cleared, 1)
            sp.dma_start(src_i[0:P - 1, :], src[0:(P - 1) * EP].rearrange("(p t) -> p t", t=EP)).then_inc(src_loaded, 16)
            sp.dma_start(src_i[P - 1:P, 0:TAIL], src[(P - 1) * EP:E].rearrange("(p t) -> p t", p=1)).then_inc(src_loaded, 16)

            def load_block(base, u):
                nb, r = base + u, u % RING
                after(sp, x_turned, nb - RING + 1)
                sp.dma_start(x_in[:, r, :], x[bass.ds(nb * P, P), :]).then_inc(x_loaded[r], 16)

            def store_block(base, u):
                nb, r = base + u - 6, (u - 6) % RING
                sp.wait_ge(dst_read, nb + 1)
                sp.dma_start(dst_table[bass.ds(nb * P, P), :], dst_out[:, r, :]).then_inc(dst_stored[r], 16)

            def blocks_step(base, u):
                if live(base, u, 0, EARLY):
                    load_block(base, u)
                if live(base, u, 6, EARLY):
                    store_block(base, u)
                if base == 0 and u == 5:
                    sp.wait_ge(cleared, 4)
                    sp.dma_start(shared[0:P - 1, :], edge_attr[0:(P - 1) * EP, :].rearrange("(p t) a -> p (t a)", t=EP)).then_inc(attr_loaded, 16)
                    sp.dma_start(shared[P - 1:P, 0:TAIL * A], edge_attr[(P - 1) * EP:E, :].rearrange("(p t) a -> p (t a)", p=1)).then_inc(attr_loaded, 16)
                    sp.dma_start(dst_i[0:P - 1, :], dst[0:(P - 1) * EP].rearrange("(p t) -> p t", t=EP)).then_inc(dst_loaded, 16)
                    sp.dma_start(dst_i[P - 1:P, 0:TAIL], dst[(P - 1) * EP:E].rearrange("(p t) -> p t", p=1)).then_inc(dst_loaded, 16)

            steps(sp, 6, blocks_step, EARLY)

            sp.wait_ge(w_cleared, 1)
            sp.wait_ge(w_split, 5)
            for h, row in enumerate((0, KR)):
                for n, k in enumerate((0, 1, 2, 0, 1, 0)):
                    sp.dma_start(w_stack[row + n * A:row + (n + 1) * A, h, :], w_parts[0:A, k, :]).then_inc(w_stacked, 16)

            def late_load(i, h, rows=P):
                nb = i * 2 + (EARLY + h)
                sp.wait_ge(x_turned, nb - 1)
                sp.dma_start(x_in[0:rows, h, :], x[bass.ds(nb * P, rows), :]).then_inc(late_x_loaded[h], 16)

            def late_store(i, h):
                nb = i * 2 + (EARLY + h)
                sp.wait_ge(dst_read, nb + 1)
                sp.dma_start(dst_table[bass.ds(nb * P, P), :], dst_out[:, h, :]).then_inc(late_dst_stored[h], 16)

            LATE = (NB - EARLY) // 2
            sp.wait_ge(x_turned, EARLY)
            for h in range(2):
                late_load(0, h)
            with sp.Fori(0, LATE - 2) as i:
                for h in range(2):
                    late_store(i, h)
                    late_load(i + 1, h)
            for h in range(2):
                late_store(LATE - 2, h)
                late_load(LATE - 1, h, P if h == 0 else LAST)
            for h in range(2):
                late_store(LATE - 1, h)

            for i in range(2):
                sp.wait_ge(scattered[i], 16 * EP // 2)
            rec_in = records[0:SPARE, :].rearrange("(g p j) c -> g p (j c)", p=P, j=G)

            def load_records(base, u):
                g, r = base + u, u % RING
                after(sp, z_added, g - RING + 1)
                sp.dma_start(rec[:, r, :, :].rearrange("p j c -> p (j c)"),
                             rec_in[bass.ds(g, 1)].rearrange("g p w -> (g p) w")).then_inc(rec_loaded[r], 16)

            steps(sp, 0, load_records)

            sp.wait_ge(z_done, GROUPS)
            sp.dma_start(xs[:, 0:(NB - 1) * D].rearrange("p (b d) -> p b d", d=D),
                         x[0:(NB - 1) * P, :].rearrange("(b p) d -> p b d", p=P)).then_inc(xs_loaded, 16)
            sp.dma_start(xs[0:LAST, (NB - 1) * D:NB * D], x[(NB - 1) * P:N, :]).then_inc(xs_loaded, 16)
            for c in range(NCH):
                sp.wait_ge(f_out, c + 1)
                sp.wait_ge(act_out, c + 1)
                b0, b1 = c * CB, min((c + 1) * CB, NB - 1)
                sp.dma_start(out[b0 * P:b1 * P, :].rearrange("(b p) d -> p b d", p=P),
                             agg[:, b0 * D:b1 * D].rearrange("p (b d) -> p b d", d=D)).then_inc(out_stored, 16)
            sp.dma_start(out[(NB - 1) * P:N, :], agg[0:LAST, (NB - 1) * D:NB * D]).then_inc(out_stored, 16)
            sp.wait_ge(out_stored, 16 * (NCH + 1))

        @block.gpsimd
        def _(pool):
            pool.iota(node_iota[:, :], pattern=[[1, P]], base=0, channel_multiplier=0,
                      allow_small_or_imprecise_dtypes=True).then_inc(consts_ready, 1)
            pool.iota(tile_iota[:, :], pattern=[[1, T]], base=0, channel_multiplier=0,
                      allow_small_or_imprecise_dtypes=True).then_inc(consts_ready, 1)
            pool.iota(pos[:, :], pattern=[[1, EP]], base=SPARE - TAIL, channel_multiplier=0,
                      allow_small_or_imprecise_dtypes=True).then_inc(consts_ready, 1)
            pool.memset(ones[:, :], 1.0).then_inc(consts_ready, 1)
            pool.memset(stage_bf[:, :, :, LO + 1:LO + 2], 0.0).then_inc(consts_ready, 1)
            pool.memset(w_stack[:, :, :], 0.0).then_inc(w_cleared, 1)
            pool.wait_ge(consts_ready, 5)
            pool.affine_select(out=ident[:, :], in_=ones[:, :], compare_op=ALU.is_equal, fill=0.0, base=0,
                               pattern=[[-1, P]], channel_multiplier=1).then_inc(consts_ready, 1)
            pool.affine_select(out=below[:, :], in_=ones[:, :], compare_op=ALU.is_gt, fill=0.0, base=0,
                               pattern=[[1, P]], channel_multiplier=-1).then_inc(consts_ready, 1)
            pool.affine_select(out=upto[:, :], in_=ones[:, :], compare_op=ALU.is_ge, fill=0.0, base=0,
                               pattern=[[1, P]], channel_multiplier=-1).then_inc(consts_ready, 1)

            pool.wait_ge(gate_turned, 4)
            pool.tensor_copy(w_parts[:, 0, :], w_edge[:, :]).then_inc(w_split, 1)
            pool.wait_ge(w_split, 1)
            pool.tensor_tensor(w_edge[:, :], w_edge[:, :], w_parts[:, 0, :], ALU.subtract).then_inc(w_split, 1)
            pool.wait_ge(w_split, 2)
            pool.tensor_copy(w_parts[:, 1, :], w_edge[:, :]).then_inc(w_split, 1)
            pool.wait_ge(w_split, 3)
            pool.tensor_tensor(w_edge[:, :], w_edge[:, :], w_parts[:, 1, :], ALU.subtract).then_inc(w_split, 1)
            pool.wait_ge(w_split, 4)
            pool.tensor_copy(w_parts[:, 2, :], w_edge[:, :]).then_inc(w_split, 1)

            def split_table(base, u):
                s = base + u
                if live(base, u, 2, EARLY):
                    pool.wait_ge(src_read, s - 1)
                    pool.tensor_tensor(src_rest[:, u % 2, :], src_rest[:, u % 2, :], src_part(s - 2, 0), ALU.subtract).then_inc(rest_ready, 1)
                if live(base, u, 3, EARLY):
                    pool.wait_ge(middle_ready, s - 2)
                    pool.tensor_tensor(src_part(s - 3, 2), src_rest[:, (u - 3) % 2, :], src_part(s - 3, 1), ALU.subtract).then_inc(low_ready, 1)

            steps(pool, 3, split_table, EARLY)

            pool.wait_ge(filled, 16 * FILL)

            with pool.Fori(0, STAGES // 2) as i:
                for h in range(2):
                    pool.wait_ge(parts_staged, i * 6 + (h * 3 + 3))
                    pool.sem_inc(taken_up, 1)
                    for c in range(CH):
                        pool.indirect_dma_start(
                            out=records, out_offset=bass.IndirectOffsetOnAxis(ap=stage_row[:, h, c:c + 1], axis=0),
                            in_=stage[:, h, c, :], in_offset=None).then_inc(scattered[h], 16)

            def gather(g, r, it):
                pool.wait_ge(rec_loaded[r], it)
                pool.sem_inc(taken_up, 1)
                for j in range(G):
                    pool.indirect_dma_start(
                        out=dst_rows[:, r, j, :], out_offset=None, in_=dst_table,
                        in_offset=bass.IndirectOffsetOnAxis(ap=rec[:, r, j, DST:DST + 1].bitcast(I32), axis=0),
                    ).then_inc(gathered[r], 16)

            for r in range(RING):
                pool.wait_ge(dst_stored[r], 16 * ((EARLY - r - 1) // RING + 1))
            for h in range(2):
                pool.wait_ge(late_dst_stored[h], 16 * ((NB - EARLY) // 2))

            with pool.Fori(0, GROUPS // RING) as it:
                for r in range(RING):
                    gather(it * RING + r, r, it * 16 + 16)

            def chunk(a, c):
                return a[:, c * CW:(c + 1) * CW]

            def node_scales(c):
                nodes = slice(c * CB, (c + 1) * CB)
                pool.wait_ge(mv_ready, 2 * c + 2)
                pool.wait_ge(f_rstd, 2 * c + 2)
                newton_step(pool, nc.gpsimd, node_rstd[:, nodes], node_var[:, nodes], node_newton[:, nodes], node_newton_done, 4 * c)
                pool.tensor_tensor(node_shift[:, nodes], node_mv[:, nodes, 0], node_rstd[:, nodes], ALU.mult).then_inc(node_product, 1)
                pool.wait_ge(node_product, c + 1)
                pool.tensor_scalar(node_shift[:, nodes], node_shift[:, nodes], -1.0, None, ALU.mult).then_inc(f_shift, 1)

            pool.wait_ge(xs_loaded, 32)
            pool.wait_ge(gb_ready, 1)
            for c in range(NCH):
                pool.tensor_tensor(chunk(x_beta, c).rearrange("p (b d) -> p b d", d=D), chunk(xs, c).rearrange("p (b d) -> p b d", d=D),
                                   gb[:, D:D2].unsqueeze(1).to_broadcast([P, CB, D]), ALU.add).then_inc(x_beta_ready, 1)
            for c in range(NCH):
                pool.wait_ge(f_log, c + 1)
                pool.tensor_tensor(chunk(sq, c), chunk(sq, c), chunk(xs, c), ALU.add).then_inc(softplus_x, 1)
                if c >= LN_LAG:
                    node_scales(c - LN_LAG)
            for c in range(NCH - LN_LAG, NCH):
                node_scales(c)

        @block.scalar
        def _(act):
            for k, (w, b) in enumerate(((gate_w, gate_b), (cand_w, cand_b))):
                cols = slice(k * D, (k + 1) * D)
                act.dma_start(w_src[:, cols], w[0:D, :]).then_inc(weights_loaded, 16)
                act.dma_start(w_dst[:, cols], w[D:2 * D, :]).then_inc(weights_loaded, 16)
                act.dma_start(w_edge[0:A, cols], w[2 * D:2 * D + A, :]).then_inc(weights_loaded, 16)
                act.dma_start(bias_row[:, cols], b.rearrange("(a d) -> a d", a=1)).then_inc(weights_loaded, 16)
            act.dma_start(gamma_row[:, 0:D], gamma.rearrange("(a d) -> a d", a=1)).then_inc(weights_loaded, 16)
            act.dma_start(gamma_row[:, D:D2], beta.rearrange("(a d) -> a d", a=1)).then_inc(weights_loaded, 16)
            act.wait_ge(weights_loaded, 160)
            for w in (w_src, w_dst, w_edge, bias_row):
                nc.scalar.activation(w[:, 0:D], w[:, 0:D], ACT.Copy, scale=-1.0).then_inc(gate_turned, 1)

            act.wait_ge(cleared, 3)
            rec_fill = records[0:SPARE, :].rearrange("(i p r) c -> i p (r c)", p=P, r=FROWS)

            def evacuate(base, u):
                s = base + u
                if s < FILL:
                    act.dma_start(rec_fill[s], fill[:, :, :].rearrange("p r c -> p (r c)")).then_inc(filled, 16)
                if live(base, u, 0, EARLY):
                    b = u % 2
                    act.wait_ge(x_turned, s + 1)
                    after(act, maps_done, s - 1)
                    nc.scalar.copy(x_t[:, b, :], sum_ps[:, b, 0:P]).then_inc(x_t_ready, 1)
                if live(base, u, 2, EARLY):
                    nb, b, r = s - 2, u % 2, (u - 2) % RING
                    act.wait_ge(maps_done, s - 1)
                    after(act, low_ready, s - 3)
                    nc.scalar.copy(src_rest[:, b, :], src_ps(b))
                    nc.scalar.copy(src_part(nb, 0), src_ps(b)).then_inc(src_read, 1)
                    if live(base, u, 2 + RING, EARLY + RING):
                        act.wait_ge(dst_stored[r], fills(base, u, 2 + RING, 16))
                    nc.scalar.copy(dst_out[:, r, :], dst_ps(b)).then_inc(dst_read, 1)
                if live(base, u, 3, EARLY):
                    act.wait_ge(rest_ready, s - 2)
                    nc.scalar.copy(src_part(s - 3, 1), src_rest[:, (u - 3) % 2, :]).then_inc(middle_ready, 1)

            steps(act, 3, evacuate, EARLY)

            act.wait_ge(dst_loaded, 32)

            def stage_columns(t0, h, i):
                after(act, scattered[h], i * (16 * CH))
                cols = bass.ds(t0, CH)

                def part(first, copies, value):
                    act.wait_ge(attr_ps_ready, value)
                    nc.scalar.copy(stage_bf[:, h, :, first * A:(first + copies) * A].rearrange("p t (k a) -> p t k a", a=A),
                                   (attr_ps, hot_ps)[h][:, 0:CH * A].rearrange("p (t a) -> p t a", a=A).unsqueeze(2)
                                   .to_broadcast([P, CH, copies, A])).then_inc(parts_staged, 1)

                part(0, 3, i * 6 + (3 * h + 1))
                nc.scalar.copy(stage_bf[:, h, :, LO:LO + 1].rearrange("p t c -> p (t c)"), lo_f[:, cols])
                nc.scalar.copy(stage[:, h, :, DST:DST + 1].bitcast(I32).rearrange("p t c -> p (t c)"), dst_i[:, cols])
                nc.scalar.copy(stage_row[:, h, :], row_i[:, cols])
                part(3, 2, i * 6 + (3 * h + 2))
                part(5, 1, i * 6 + (3 * h + 3))

            def late_block(i, h, rows=P):
                nb = i * 2 + (EARLY - STAGES1 + h)
                act.wait_ge(x_turned, nb + 1)
                act.wait_ge(maps_done, nb)
                nc.scalar.copy(x_t[:, h, 0:rows], sum_ps[:, h, 0:rows]).then_inc(x_t_ready, 1)
                act.wait_ge(maps_done, nb + 1)
                act.wait_ge(low_ready, nb)
                nc.scalar.copy(src_rest[:, h, :], src_ps(h))
                nc.scalar.copy(src_part(nb, 0), src_ps(h)).then_inc(src_read, 1)
                after(act, late_dst_stored[h], i * 16 - STAGES1 // 2 * 16)
                nc.scalar.copy(dst_out[:, h, :], dst_ps(h)).then_inc(dst_read, 1)
                act.wait_ge(rest_ready, nb + 1)
                nc.scalar.copy(src_part(nb, 1), src_rest[:, h, :]).then_inc(middle_ready, 1)

            for k in range(STAGES1):
                if k in PIECES:
                    act.wait_ge(rows_ready, PIECES.index(k) + 1)
                stage_columns(k * CH, k % 2, k // 2)
            for r in range(RING):
                act.wait_ge(dst_stored[r], 16 * ((EARLY - r - 1) // RING + 1))

            def later_stages(i, last=P):
                for h in range(2):
                    stage_columns(i * (2 * CH) + h * CH, h, i)
                    late_block(i, h, last if h else P)

            later_stages(STAGES1 // 2)
            act.wait_ge(rows_ready, len(PIECES) - 1)
            with act.Fori(STAGES1 // 2 + 1, STAGES // 2 - 1) as i:
                later_stages(i)
            later_stages(STAGES // 2 - 1, LAST)

            nc.scalar.preload_act_table_set("natural_log_exp_and_others")

            def step(base, u):
                s = base + u
                b = (u - 1) % 2

                def log_part(n, to, source, function, **scaling):
                    if live(base, u, 3):
                        act.wait_ge(*((logs_ready, s * 3 + (n - 9)) if n else (last_z_copied, s - 2)))
                        nc.scalar.activation(to[:, b, :], source[:, b, :], function, **scaling).then_inc(logs_ready, 1)

                if live(base, u, 3):
                    after(act, parts_ready, s - 4)
                    act.wait_ge(z_added, s - 2)
                    nc.scalar.copy(z[:, b, LAST_Z], z_ps[:, b, LAST_Z]).then_inc(last_z_copied, 1)
                if live(base, u, 1):
                    act.wait_ge(turned, s)
                    after(act, z_done, s - 2)
                    nc.scalar.copy(hot_t[:, b, :], hot_ps[:, :])
                log_part(0, neg, z, ACT.Abs)
                if live(base, u, 1):
                    nc.scalar.copy(attr_t[:, b, :], attr_ps[:, 0:G // 2 * P]).then_inc(hot_t_ready, 1)
                log_part(1, neg, neg, ACT.Exp, scale=-1.0)
                if live(base, u, 4):
                    act.wait_ge(parts_ready, s - 3)
                    gate = parts[:, (u - 4) % 2, :].rearrange("p (j d) -> p j d", d=D2)[:, :, 0:D]
                    nc.scalar.activation(gate, gate, ACT.Exp, scale=-1.0).then_inc(gate_ready, 1)
                log_part(2, neg, neg, ACT.Ln, bias=1.0)

            steps(act, 4, step)

            for c in range(NCH):
                act.wait_ge(centered, c + 1)
                if c == 0:
                    act.wait_ge(col_sum, 1)
                nc.scalar.activation(sq[:, c * CW:(c + 1) * CW], agg[:, c * CW:(c + 1) * CW], ACT.Square).then_inc(squared, 1)
            act.wait_ge(var_ready, 1)
            nc.scalar.activation(rstd[:, :], var, ACT.Ln).then_inc(rstd_ready, 1)
            act.wait_ge(rstd_ready, 1)
            nc.scalar.activation(rstd[:, :], rstd[:, :], ACT.Exp, scale=-0.5).then_inc(rstd_ready, 1)
            act.wait_ge(sq_sum, 1)
            act.wait_ge(part_sq, 1)
            for c in range(NCH + LN_LAG + 1):
                if c < NCH:
                    part = sq[:, c * CW:(c + 1) * CW]
                    act.wait_ge(t_ready, c + 1)
                    nc.scalar.activation(part, agg[:, c * CW:(c + 1) * CW], ACT.Abs).then_inc(f_abs, 1)
                    act.wait_ge(f_abs, c + 1)
                    nc.scalar.activation(part, part, ACT.Exp, scale=-1.0).then_inc(f_exp, 1)
                    act.wait_ge(f_exp, c + 1)
                    nc.scalar.activation(part, part, ACT.Ln, bias=1.0).then_inc(f_log, 1)
                d = c - LN_LAG
                if 0 <= d < NCH:
                    nodes = node_rstd[:, d * CB:(d + 1) * CB]
                    act.wait_ge(mv_ready, 2 * d + 2)
                    nc.scalar.activation(nodes, node_var[:, d * CB:(d + 1) * CB], ACT.Ln).then_inc(f_rstd, 1)
                    act.wait_ge(f_rstd, 2 * d + 1)
                    nc.scalar.activation(nodes, nodes, ACT.Exp, scale=-0.5).then_inc(f_rstd, 1)
                if 1 <= d:
                    act.wait_ge(f_shift, d)
                    for b in range(d * CB - ACT_OUT, d * CB):
                        part = agg[:, b * D:(b + 1) * D]
                        last = nc.scalar.activation(part, part, ACT.Identity, scale=node_rstd[:, b:b + 1],
                                                    bias=node_shift[:, b:b + 1])
                    last.then_inc(act_out, 1)

        @block.vector
        def _(dve):
            v = nc.vector
            v.memset(src_i[96:P, TAIL:EP], NB * P).then_inc(cleared, 1)
            v.memset(dst_i[96:P, TAIL:EP], 0).then_inc(cleared, 1)
            v.memset(fill[:, :, :], 0.0).then_inc(nstep, 1)
            dve.wait_ge(nstep, 1)
            v.memset(fill.bitcast(BF16)[:, :, LO:LO + 1], -1.0).then_inc(cleared, 1)
            v.memset(shared[96:P, TAIL * A:EP * A], 0.0).then_inc(cleared, 1)

            dve.wait_ge(src_loaded, 32)
            v.tensor_scalar(row_i[:, :], src_i[:, :], 7, None, ALU.logical_shift_right).then_inc(src_split, 1)
            dve.wait_ge(src_split, 1)
            v.tensor_copy(hi_f[:, :], row_i[:, :]).then_inc(src_split, 1)
            dve.wait_ge(src_split, 2)
            dve.wait_ge(consts_ready, 8)
            def count_seven(b0):
                for k in range(7):
                    b = b0 + k
                    after(dve, counted, b - 1 if k else b)
                    v.tensor_scalar(eqb[:, BUF[k], :], hi_f[:, :], node_iota[:, bass.ds(b, 1)], 0.0, ALU.is_equal, ALU.add,
                                    accum_out=count[:, bass.ds(b, 1)]).then_inc(counted, 1)

            count_seven(0)
            with dve.Fori(1, NB // 7) as i:
                count_seven(i * 7)
            v.tensor_scalar(lo_i[:, :], src_i[:, :], P - 1, None, ALU.bitwise_and).then_inc(src_split, 1)
            v.tensor_copy(ident_bf[:, :], ident[:, :]).then_inc(idents_ready, 1)
            v.tensor_scalar(minus_ident[:, :], ident[:, :], -1.0, None, ALU.mult).then_inc(idents_ready, 1)
            dve.wait_ge(src_split, 3)
            v.tensor_copy(lo_f[:, :], lo_i[:, :]).then_inc(src_split, 1)
            dve.wait_ge(base_ps, 1)
            v.tensor_scalar(total_f[:, :], attr_ps[0:NB, NB:NB + 1], float(P - 1), None, ALU.add).then_inc(base_step, 1)
            dve.wait_ge(base_step, 1)
            v.tensor_copy(total_i[:, :], total_f[:, :]).then_inc(base_step, 1)
            dve.wait_ge(base_step, 2)
            v.tensor_scalar(total_i[:, :], total_i[:, :], 7, None, ALU.logical_shift_right).then_inc(base_step, 1)
            dve.wait_ge(base_step, 3)
            v.tensor_copy(block_tiles[:, :], total_i[:, :]).then_inc(base_step, 1)
            dve.wait_ge(base_step, 4)
            v.tensor_scalar(tiles_below[:, :], below[0:NB, 0:NB], block_tiles[:, 0:1], None, ALU.mult).then_inc(base_step, 1)
            dve.wait_ge(base_ps, 2)
            v.tensor_scalar(first[:, :], attr_ps[:, 256:256 + NB], float(P), -1.0, ALU.mult, ALU.add).then_inc(base_step, 1)
            v.tensor_copy(block_end[:, :], attr_ps[0:NB, 256 + NB:257 + NB]).then_inc(base_step, 1)
            dve.wait_ge(base_step, 7)
            v.tensor_tensor(first[:, :], first[:, :], attr_ps[:, 0:NB], ALU.add).then_inc(base_step, 1)
            v.tensor_scalar(begun[:, :], tile_iota[:, :], block_end[:, 0:1], None, ALU.is_ge).then_inc(base_step, 1)
            dve.wait_ge(base_step, 9)

            for n in range(len(PIECES) - 1):
                t0, t1 = PIECES[n] * CH, PIECES[n + 1] * CH
                w = t1 - t0

                def equal(b, k):
                    v.tensor_scalar(eq[:, k, t0:t1], hi_f[:, t0:t1], node_iota[:, bass.ds(b, 1)], None,
                                    ALU.is_equal).then_inc(eq_done, 1)

                def place_seven(b0):
                    for k in range(7):
                        b, m = b0 + k, BUF[k]
                        dve.wait_ge(eq_done, b + (n * (NB + 1) + 1))
                        v.tensor_tensor_scan(cum[:, m, t0:t1], eq[:, m, t0:t1], eq[:, m, t0:t1], first[:, bass.ds(b, 1)],
                                             ALU.add, ALU.bypass).then_inc(scan_done, 1)
                        after(dve, placed, b + n * NB)
                        equal(b + 1, BUF[(k + 1) % 7])
                        dve.wait_ge(scan_done, b + (n * NB + 1))
                        v.tensor_scalar(first[:, bass.ds(b, 1)], cum[:, m, t1 - 1:t1], 0.0, None, ALU.add)
                        v.copy_predicated(pos[:, t0:t1], eq[:, m, t0:t1], cum[:, m, t0:t1]).then_inc(placed, 1)

                equal(0, 0)
                if n == 0:
                    place_seven(0)
                with dve.Fori(1 if n == 0 else 0, NB // 7) as i:
                    place_seven(i * 7)
                dve.wait_ge(placed, (n + 1) * NB)
                if n == 0:
                    dve.wait_ge(src_split, 4)
                done = n * 6 - 1
                v.tensor_copy(row_i[:, t0:t1], pos[:, t0:t1]).then_inc(nstep, 1)
                dve.wait_ge(nstep, done + 3)
                v.tensor_scalar(src_i[:, t0:t1], row_i[:, t0:t1], P - 1, GH, ALU.bitwise_and, ALU.logical_shift_left).then_inc(nstep, 1)
                v.tensor_scalar(lo_i[:, t0:t1], row_i[:, t0:t1], 7, G - 1, ALU.logical_shift_right, ALU.bitwise_and).then_inc(nstep, 1)
                v.tensor_scalar(row_i[:, t0:t1], row_i[:, t0:t1], 7 + GH, 7 + GH, ALU.logical_shift_right, ALU.logical_shift_left).then_inc(nstep, 1)
                dve.wait_ge(nstep, done + 6)
                v.tensor_tensor(row_i[:, t0:t1], row_i[:, t0:t1], src_i[:, t0:t1], ALU.bitwise_or).then_inc(nstep, 1)
                dve.wait_ge(nstep, done + 7)
                v.tensor_tensor(row_i[:, t0:t1], row_i[:, t0:t1], lo_i[:, t0:t1], ALU.bitwise_or).then_inc(nstep, 1)
                dve.wait_ge(nstep, done + 8)
                dve.sem_inc(rows_ready, 1)
                if n == len(PIECES) - 2:
                    v.memset(agg[:, :], 0.0).then_inc(nstep, 1)
                    dve.wait_ge(base_ps, 3)
                    v.tensor_scalar(tile_block[:, :, :].rearrange("p (k g) j -> p k (g j)", k=2), sum_ps[0:1, :, 0:T // 2], float(NB - 1),
                                    None, ALU.min).then_inc(packing, 1)
                    acc = tile_block[:, :, G - 1]
                    for k, j in enumerate(range(G - 2, -1, -1)):
                        dve.wait_ge(packing, k + 1)
                        v.scalar_tensor_tensor(out=packed[:, :], in0=acc, scalar=float(1 << BITS), in1=tile_block[:, :, j],
                                               op0=ALU.mult, op1=ALU.add).then_inc(packing, 1)
                        acc = packed[:, :]
                    dve.wait_ge(packing, G)
                    v.tensor_copy(group_blocks[:, :], packed[:, :]).then_inc(tile_blocks_ready, 1)
                    dve.wait_ge(gb_ps, 1)
                    v.tensor_copy(gb[:, :], sum_ps[:, 0, 0:D2]).then_inc(gb_ready, 1)

            with dve.Fori(0, (NB - EARLY) // 2) as i:
                for h in range(2):
                    nb = i * 2 + (EARLY + h)
                    dve.wait_ge(src_read, nb + 1)
                    v.tensor_tensor(src_rest[:, h, :], src_rest[:, h, :], src_part(nb, 0), ALU.subtract).then_inc(rest_ready, 1)
                    dve.wait_ge(middle_ready, nb + 1)
                    v.tensor_tensor(src_part(nb, 2), src_rest[:, h, :], src_part(nb, 1), ALU.subtract).then_inc(low_ready, 1)

            def step(base, u):
                s = base + u
                if live(base, u, 7):
                    at = blocks_of(mybir.EngineType.DVE, s - 7)

                def add_sum(j):
                    if live(base, u, 7):
                        if j == 0:
                            dve.wait_ge(summed, s - 6)
                        else:
                            dve.wait_ge(agg_added, (s - 7) * G + j)
                        part = agg[:, bass.ds(at[j] * D, D)]
                        v.tensor_tensor(part, part, sum_ps[:, (u - 7) % 2, j * D:(j + 1) * D], ALU.add).then_inc(agg_added, 1)

                if live(base, u, 3):
                    r, b = (u - 3) % RING, (u - 3) % 2
                    dve.wait_ge(gathered[r], fills(base, u, 3, 16 * G))
                    dve.wait_ge(z_full, s - 2)
                    after(dve, parts_ready, s - 4)
                    v.tensor_tensor(z[:, b, 0:(G - 1) * D2], z_ps[:, b, 0:(G - 1) * D2],
                                    dst_rows[:, r, 0:G - 1, :].rearrange("p j d -> p (j d)"), ALU.add).then_inc(z_added, 1)
                if live(base, u, 7):
                    after(dve, agg_added, (s - 7) * G)
                add_sum(0)
                if live(base, u, 0):
                    r = u % RING
                    dve.wait_ge(rec_loaded[r], fills(base, u, 0, 16))
                    after(dve, summed, s - OHR + 1)
                    v.tensor_tensor(hot[:, u, :].rearrange("p (j n) -> p j n", n=P),
                                    node_iota[:, :].unsqueeze(1).to_broadcast([P, G, P]),
                                    rec_bf[:, r, :, LO:LO + 1].to_broadcast([P, G, P]), ALU.is_equal).then_inc(hot_ready, 1)
                add_sum(1)
                if live(base, u, 4):
                    b = (u - 4) % 2
                    dve.wait_ge(logs_ready, s * 3 - 9)
                    after(dve, message_ready, s - 5)
                    v.scalar_tensor_tensor(out=parts[:, b, :], in0=z[:, b, :], scalar=0.0, in1=neg[:, b, :], op0=ALU.max,
                                           op1=ALU.add).then_inc(parts_ready, 1)
                add_sum(2)
                if live(base, u, 5):
                    b = (u - 5) % 2
                    dve.wait_ge(gate_ready, s - 4)
                    after(dve, summed, s - 6)
                    halves = parts[:, b, :].rearrange("p (j d) -> p j d", d=D2)
                    v.tensor_tensor(message[:, b, :].rearrange("p (j d) -> p j d", d=D), halves[:, :, 0:D],
                                    halves[:, :, D:D2], ALU.mult).then_inc(message_ready, 1)
                add_sum(3)

            steps(dve, 7, step)

            def blocks(a, c):
                return a[:, c * CW:(c + 1) * CW].rearrange("p (b d) -> p b d", d=D)

            def over_blocks(a, b0, b1):
                return a[:, b0 * D:b1 * D].rearrange("p (b d) -> p d b", d=D)

            def every_block(a):
                return a.unsqueeze(1).to_broadcast([P, CB, D])

            dve.wait_ge(agg_added, T)
            v.tensor_reduce(rstd[:, :], over_blocks(agg, PE_BLOCKS, NB), AX_X, ALU.add).then_inc(part_sum, 1)
            dve.wait_ge(col_sum, 1)
            v.tensor_reduce(mean[:, :], sum_ps[:, 0, :].rearrange("p (c f) -> p f c", f=D), AX_X, ALU.add).then_inc(mean_ready, 1)
            dve.wait_ge(mean_ready, 1)
            v.tensor_scalar(mean[:, :], mean[:, :], 1.0 / N, None, ALU.mult).then_inc(mean_ready, 1)
            dve.wait_ge(mean_ready, 2)
            for c in range(NCH):
                v.tensor_tensor(blocks(agg, c), blocks(agg, c), every_block(mean[:, :]), ALU.subtract).then_inc(centered, 1)
            dve.wait_ge(squared, NCH)
            v.tensor_reduce(mean[:, :], over_blocks(sq, PE_SQUARES, NB - 1), AX_X, ALU.add).then_inc(part_sq, 1)
            dve.wait_ge(sq_sum, 1)
            v.tensor_reduce(rstd[:, :], sum_ps[:, 1, :].rearrange("p (c f) -> p f c", f=D), AX_X, ALU.add).then_inc(var_sum, 1)
            dve.wait_ge(var_sum, 1)
            v.tensor_scalar(var, rstd[:, :], 1.0 / N, BN_EPS, ALU.mult, ALU.add).then_inc(var_ready, 1)
            dve.wait_ge(rstd_ready, 2)
            dve.wait_ge(var_ready, 1)
            newton_step(dve, v, rstd[:, :], var, newton, newton_done, 0)
            v.tensor_tensor(rstd[:, :], rstd[:, :], gb[:, 0:D], ALU.mult).then_inc(rstd_ready, 1)
            dve.wait_ge(rstd_ready, 3)
            for c in range(NCH + 1):
                if c < NCH:
                    a = blocks(agg, c)
                    v.tensor_tensor(a, a, every_block(rstd[:, :]), ALU.mult).then_inc(scaled, 1)
                if c > 0:
                    a = blocks(agg, c - 1)
                    dve.wait_ge(scaled, c)
                    dve.wait_ge(x_beta_ready, c)
                    v.tensor_tensor(a, a, blocks(x_beta, c - 1), ALU.add).then_inc(t_ready, 1)

            for c in range(NCH + 2):
                if c < NCH:
                    nodes = slice(c * CB, (c + 1) * CB)
                    dve.wait_ge(softplus_x, c + 1)
                    v.scalar_tensor_tensor(out=blocks(agg, c), in0=blocks(agg, c), scalar=0.0, in1=blocks(sq, c), op0=ALU.max,
                                           op1=ALU.add).then_inc(y_ready, 1)
                    dve.wait_ge(y_ready, c + 1)
                    for b in range(c * CB, (c + 1) * CB):
                        last = v.bn_stats(node_stats[:, b, :], agg[:, b * D:(b + 1) * D])
                    last.then_inc(stats_ready, 1)
                    dve.wait_ge(stats_ready, c + 1)
                    for b in range(c * CB, (c + 1) * CB):
                        last = v.bn_aggr(node_mv[:, b, :], node_stats[:, b, :])
                    last.then_inc(mv_ready, 1)
                    dve.wait_ge(mv_ready, 2 * c + 1)
                    v.tensor_scalar(node_var[:, nodes], node_mv[:, nodes, 1], LN_EPS, None, ALU.add).then_inc(mv_ready, 1)
                if c > 1:
                    d = c - 2
                    dve.wait_ge(f_shift, d + 1)
                    for b in range(d * CB, (d + 1) * CB - ACT_OUT):
                        part = agg[:, b * D:(b + 1) * D]
                        last = v.tensor_scalar(part, part, node_rstd[:, b:b + 1], node_shift[:, b:b + 1], ALU.mult, ALU.add)
                    last.then_inc(f_out, 1)

        @block.tensor
        def _(pe):
            def tables(base, u):
                s = base + u
                if live(base, u, 0, EARLY):
                    r, b = u % RING, u % 2
                    pe.wait_ge(x_loaded[r], fills(base, u, 0, 16))
                    after(pe, x_t_ready, s - 1)
                    pe.transpose(sum_ps[:, b, 0:P], x_in[:, r, :], ident[:, :]).then_inc(x_turned, 1)
                if live(base, u, 1, EARLY):
                    b = (u - 1) % 2
                    pe.wait_ge(x_t_ready, s)
                    after(pe, src_read, s - 2)
                    after(pe, dst_read, s - 2)
                    pe.matmul(src_ps(b), x_t[:, b, :], w_src[:, :], start=True, stop=False)
                    pe.matmul(src_ps(b), ones[0:1, :], bias_row[:, :], start=False, stop=True)
                    pe.matmul(dst_ps(b), x_t[:, b, :], w_dst[:, :], start=True, stop=True).then_inc(maps_done, 1)

            def ranks_start():
                pe.wait_ge(counted, NB)
                pe.matmul(attr_ps[:, 0:NB], below[:, :], count[:, :], start=True, stop=True)
                pe.matmul(attr_ps[0:NB, NB:NB + 1], count[:, :], ones[:, 0:1], start=True, stop=True).then_inc(base_ps, 1)
                pe.wait_ge(base_step, 5)
                pe.matmul(attr_ps[:, 256:256 + NB], ones[0:NB, :], tiles_below[:, :], start=True, stop=True)
                pe.matmul(attr_ps[0:NB, 256 + NB:257 + NB], upto[0:NB, 0:NB], block_tiles[:, :], start=True, stop=True).then_inc(base_ps, 1)

            def early_tables(base, u):
                if base == 0 and u == 5:
                    ranks_start()
                tables(base, u)

            pe.wait_ge(consts_ready, 8)
            pe.wait_ge(weights_loaded, 160)
            pe.wait_ge(gate_turned, 4)
            steps(pe, 1, early_tables, EARLY)

            pe.wait_ge(base_step, 9)
            pe.wait_ge(x_t_ready, EARLY)
            for k in range(2):
                mm = pe.matmul(sum_ps[0:1, k, 0:T // 2], ones[0:NB, 0:1], begun[:, k * (T // 2):(k + 1) * (T // 2)],
                               start=True, stop=True)
            mm.then_inc(base_ps, 1)


            def split_columns(h, i):
                to = (attr_ps, hot_ps)[h][:, 0:CH * A]
                for k in range(3):
                    if k:
                        pe.wait_ge(parts_staged, i * 6 + (h * 3 + k))
                    else:
                        after(pe, parts_staged, i * 6 + (h * 3 - 3))
                    mm = pe.matmul(to, ident[:, :], shared[:, bass.ds(i * (2 * CH * A) + h * CH * A, CH * A)], start=True,
                                   stop=k == 0)
                    for n in range(k):
                        mm = pe.matmul(to, minus_ident[:, :], stage_bf[:, h, :, 3 * n * A:(3 * n + 1) * A], start=False,
                                       stop=n == k - 1)
                    mm.then_inc(attr_ps_ready, 1)

            def late_tables(i, h, rows=P):
                nb = i * 2 + (EARLY - STAGES1 + h)
                pe.wait_ge(late_x_loaded[h], i * 16 - (STAGES1 // 2 - 1) * 16)
                pe.transpose(sum_ps[:, h, 0:rows], x_in[0:rows, h, :], ident[0:rows, 0:rows]).then_inc(x_turned, 1)
                pe.wait_ge(x_t_ready, nb + 1)
                pe.wait_ge(src_read, nb)
                pe.wait_ge(dst_read, nb)
                pe.matmul(src_ps(h), x_t[:, h, :], w_src[:, :], start=True, stop=False)
                pe.matmul(src_ps(h), ones[0:1, :], bias_row[:, :], start=False, stop=True)
                pe.matmul(dst_ps(h), x_t[:, h, :], w_dst[:, :], start=True, stop=True).then_inc(maps_done, 1)

            pe.wait_ge(idents_ready, 2)
            pe.wait_ge(attr_loaded, 32)
            for k in range(STAGES1):
                split_columns(k % 2, k // 2)

            pe.wait_ge(tile_blocks_ready, 1)
            pe.matmul(sum_ps[:, 0, 0:D2], ones[0:1, :], gamma_row[:, :], start=True, stop=True).then_inc(gb_ps, 1)
            pe.wait_ge(gb_ready, 1)

            def later_stages(i, last=P):
                for h in range(2):
                    split_columns(h, i)
                    late_tables(i, h, last if h else P)

            with pe.Fori(STAGES1 // 2, STAGES // 2 - 1) as i:
                later_stages(i)
            later_stages(STAGES // 2 - 1, LAST)

            pe.wait_ge(low_ready, NB)
            pe.wait_ge(w_stacked, 192)

            def step(base, u):
                s = base + u
                if live(base, u, 2):
                    at = blocks_of(mybir.EngineType.PE, s - 2)
                if live(base, u, 3):
                    b, r = (u - 3) % 2, (u - 3) % RING
                    pe.wait_ge(gathered[r], fills(base, u, 3, 16 * G))
                    pe.matmul(z_ps[:, b, LAST_Z], ident[:, :], dst_rows[:, r, G - 1, :], start=False, stop=True).then_inc(z_full, 1)
                if live(base, u, 1):
                    pe.wait_ge(hot_ready, s)
                    after(pe, hot_t_ready, s - 1)
                    for j in range(G):
                        pe.transpose(hot_ps[:, j * P:(j + 1) * P], hot[:, (u - 1) % OHR, j * P:(j + 1) * P], ident[:, :])
                    for k in range(G // 2):
                        mm = pe.matmul(attr_ps[:, k * P:(k + 1) * P], rec_bf[:, (u - 1) % RING, 2 * k:2 * k + 2, :].rearrange("p j v -> p (j v)"), ident_bf[:, :],
                                       start=True, stop=True)
                    mm.then_inc(turned, 1)
                if live(base, u, 2):
                    b = (u - 2) % 2
                    pe.wait_ge(hot_t_ready, s - 1)
                    after(pe, z_added, s - 3)
                    after(pe, last_z_copied, s - 3)
                    for j in range(G):
                        to = z_ps[:, b, j * D2:(j + 1) * D2]
                        pe.matmul(to, attr_t[:, b, j // 2 * P:(j // 2 + 1) * P], w_stack[:, j % 2, :], start=True, stop=False)
                        for k in range(3):
                            mm = pe.matmul(to, hot_t[:, b, j * P:(j + 1) * P],
                                           src_parts[:, bass.ds(at[j] * (3 * D2) + k * D2, D2)], start=False,
                                           stop=k == 2 and j < G - 1)
                    mm.then_inc(z_done, 1)
                if live(base, u, 6):
                    pe.wait_ge(message_ready, s - 5)
                    after(pe, agg_added, (s - 7) * G)
                    o, b = (u - 6) % OHR, (u - 6) % 2
                    for j in range(G):
                        mm = pe.matmul(sum_ps[:, b, j * D:(j + 1) * D], hot[:, o, j * P:(j + 1) * P],
                                       message[:, b, j * D:(j + 1) * D], start=True, stop=True)
                    mm.then_inc(summed, 1)

            steps(pe, 6, step)

            def node_sums(a, blocks, to, chunk_ready=None):
                for c in range(blocks // G):
                    if chunk_ready is not None:
                        pe.wait_ge(chunk_ready, -(-(c + 1) * G // CB))
                    pe.matmul(to, ones[:, :], a[:, c * G * D:(c + 1) * G * D], start=c == 0, stop=False)

            pe.wait_ge(agg_added, T)
            node_sums(agg, PE_BLOCKS, sum_ps[:, 0, :])
            pe.wait_ge(part_sum, 1)
            pe.matmul(sum_ps[:, 0, 0:D], ones[:, :], rstd[:, :], start=False, stop=True).then_inc(col_sum, 1)
            node_sums(sq, PE_SQUARES, sum_ps[:, 1, :], squared)
            pe.wait_ge(squared, NCH)
            pe.matmul(sum_ps[:, 1, 0:D], ones[0:LAST, :], sq[0:LAST, (NB - 1) * D:NB * D], start=False, stop=False)
            pe.wait_ge(part_sq, 1)
            pe.matmul(sum_ps[:, 1, 0:D], ones[:, :], mean[:, :], start=False, stop=True).then_inc(sq_sum, 1)


_INS = ['x', 'src', 'dst', 'edge_attr_10', 'L0_gnn_gate_w', 'L0_gnn_gate_b', 'L0_gnn_cand_w', 'L0_gnn_cand_b',
        'L0_gnn_bn_gamma', 'L0_gnn_bn_beta']


def kernel(**inputs):
    import numpy as _np
    import concourse.bacc as _bacc
    from concourse import mybir as _mybir
    from concourse.bass_utils import run_bass_kernel_spmd as _run

    nc = _bacc.Bacc("TRN2", target_bir_lowering=False, num_devices=1)
    arrays, args = {}, []
    for name in _INS:
        a = _np.ascontiguousarray(inputs[name])
        arrays[f"in_{name}_dram"] = a
        args.append(nc.dram_tensor(f"in_{name}_dram", a.shape, _mybir.dt.from_np(a.dtype), kind="ExternalInput").ap())
    shape = tuple(inputs['x'].shape)
    args.append(nc.dram_tensor("out_0_dram", shape, _mybir.dt.float32, kind="ExternalOutput").ap())
    gnn_kernel(nc, *args)
    r = _run(nc, [arrays], core_ids=[0])
    return r.results[0]["out_0_dram"]
```
